# Optimizing a Trainium2 kernel written in Bass

```python
import numpy as np
import jax
import jax.numpy as jnp

def _softmax(x, axis=-1):
    return jax.nn.softmax(x, axis=axis)

def _gelu(x):
    return jax.nn.gelu(x, approximate=True)

def _silu(x):
    return jax.nn.silu(x)

def _sigmoid(x):
    return jax.nn.sigmoid(x)

def _layernorm(x, axis=-1, eps=1e-05):
    m = jnp.mean(x, axis=axis, keepdims=True)
    v = jnp.var(x, axis=axis, keepdims=True)
    return (x - m) / jnp.sqrt(v + eps)

def _scatter_add(tgt, idx, src, axis=0):
    return tgt.at[idx].add(src)

def _segment_sum(src, seg, n):
    return jax.ops.segment_sum(src, seg, n)
kernel_name = 'mk_conv_preact_d2_conv_nchw768_r4_98ecdc'

def setup_inputs(seed: int=0):
    np.random.seed(seed)
    _w = jnp.asarray

    def _rec_inputs():
        import jax
        import jax.numpy as jnp
        _gk = jax.random.key(seed)
        x = 0.0001108 + 1 * jax.random.normal(jax.random.fold_in(_gk, 1), (16, 192, 56, 56), jnp.float32)
        return x
    x = _rec_inputs()

    def _L0_conv_setup():
        import math
        import jax, jax.numpy as jnp
        import numpy as np
        DIM = 192
        TARGET_DIM = 256

        def _hadamard_matrix(n: int) -> np.ndarray:
            H = np.array([[1.0]], dtype=np.float32)
            while H.shape[0] < n:
                H = np.block([[H, H], [H, -H]])
            return H / math.sqrt(n)
        _H = jnp.asarray(_hadamard_matrix(TARGET_DIM))
        key = jax.random.key(seed)
        x = jax.random.normal(key, (16, 192, 56, 56), dtype=jnp.float32)
        return {'x': x}
    _L0_conv_all = _L0_conv_setup()
    _L0_conv_in = {k: v for k, v in _L0_conv_all.items() if k in ()}
    del _L0_conv_all

    def _L1_conv_setup():
        import jax, jax.numpy as jnp
        import numpy as np
        DIM = 192
        EPS = 1e-06

        def _layernorm(x, gamma, beta):
            mu = jnp.mean(x, axis=-1, keepdims=True)
            var = jnp.mean(jnp.square(x - mu), axis=-1, keepdims=True)
            return (x - mu) * jax.lax.rsqrt(var + EPS) * gamma + beta
        key = jax.random.key(seed)
        ks = jax.random.split(key, 10)
        B, C, H, W = (16, DIM, 32, 32)
        s = 1.0 / np.sqrt(C)
        return {'x': jax.random.normal(ks[0], (B, C, H, W), dtype=jnp.float32), 'W1': jax.random.uniform(ks[1], (C, C), jnp.float32, -s, s), 'b1': jax.random.uniform(ks[2], (C,), jnp.float32, -s, s), 'g1': jnp.ones((C,), jnp.float32), 'beta1': jnp.zeros((C,), jnp.float32), 'W2': jax.random.uniform(ks[3], (C, C), jnp.float32, -s, s), 'b2': jax.random.uniform(ks[4], (C,), jnp.float32, -s, s), 'g2': jnp.ones((C,), jnp.float32), 'beta2': jnp.zeros((C,), jnp.float32), 'W3': jax.random.uniform(ks[5], (C, C), jnp.float32, -s, s), 'b3': jax.random.uniform(ks[6], (C,), jnp.float32, -s, s)}
    _L1_conv_all = _L1_conv_setup()
    _L1_conv_in = {k: v for k, v in _L1_conv_all.items() if k in ('W1', 'b1', 'g1', 'beta1', 'W2', 'b2', 'g2', 'beta2', 'W3', 'b3')}
    del _L1_conv_all
    return {'x': x, 'L1_conv_W1': _L1_conv_in['W1'], 'L1_conv_b1': _L1_conv_in['b1'], 'L1_conv_g1': _L1_conv_in['g1'], 'L1_conv_beta1': _L1_conv_in['beta1'], 'L1_conv_W2': _L1_conv_in['W2'], 'L1_conv_b2': _L1_conv_in['b2'], 'L1_conv_g2': _L1_conv_in['g2'], 'L1_conv_beta2': _L1_conv_in['beta2'], 'L1_conv_W3': _L1_conv_in['W3'], 'L1_conv_b3': _L1_conv_in['b3']}

def reference(x, L1_conv_W1, L1_conv_b1, L1_conv_g1, L1_conv_beta1, L1_conv_W2, L1_conv_b2, L1_conv_g2, L1_conv_beta2, L1_conv_W3, L1_conv_b3):
    import jax
    import jax.numpy as jnp

    def _L0_conv_ref(x):
        import math
        import jax, jax.numpy as jnp
        import numpy as np
        DIM = 192
        TARGET_DIM = 256

        def _hadamard_matrix(n: int) -> np.ndarray:
            H = np.array([[1.0]], dtype=np.float32)
            while H.shape[0] < n:
                H = np.block([[H, H], [H, -H]])
            return H / math.sqrt(n)
        _H = jnp.asarray(_hadamard_matrix(TARGET_DIM))
        B, C, Hs, Ws = x.shape
        xr = jnp.transpose(x, (0, 2, 3, 1)).reshape(-1, DIM)
        xp = jnp.pad(xr, ((0, 0), (0, TARGET_DIM - DIM)))
        y = xp @ _H.astype(x.dtype)
        y = y[:, :DIM]
        y = y.reshape(B, Hs, Ws, C)
        return jnp.transpose(y, (0, 3, 1, 2))

    def _L1_conv_ref(x, W1, b1, g1, beta1, W2, b2, g2, beta2, W3, b3):
        import jax, jax.numpy as jnp
        import numpy as np
        DIM = 192
        EPS = 1e-06

        def _layernorm(x, gamma, beta):
            mu = jnp.mean(x, axis=-1, keepdims=True)
            var = jnp.mean(jnp.square(x - mu), axis=-1, keepdims=True)
            return (x - mu) * jax.lax.rsqrt(var + EPS) * gamma + beta
        h = jnp.transpose(x, (0, 2, 3, 1))
        h = jnp.einsum('bhwc,oc->bhwo', h, W1) + b1
        h = jax.nn.gelu(_layernorm(h, g1, beta1), approximate=False)
        h = jnp.einsum('bhwc,oc->bhwo', h, W2) + b2
        h = jax.nn.gelu(_layernorm(h, g2, beta2), approximate=False)
        h = jnp.einsum('bhwc,oc->bhwo', h, W3) + b3
        return jnp.transpose(h, (0, 3, 1, 2))

    def _gn(v, G=32, eps=1e-05):
        B_, C_, H_, W_ = v.shape
        g = v.reshape(B_, G, C_ // G, H_, W_)
        m = jnp.mean(g, axis=(2, 3, 4), keepdims=True)
        s = jnp.var(g, axis=(2, 3, 4), keepdims=True)
        return ((g - m) / jnp.sqrt(s + eps)).reshape(v.shape)

    def _ln_c(v, eps=1e-06):
        m = jnp.mean(v, axis=1, keepdims=True)
        s = jnp.var(v, axis=1, keepdims=True)
        return (v - m) / jnp.sqrt(s + eps)

    def _ln_t(v, eps=1e-05):
        m = jnp.mean(v, axis=-1, keepdims=True)
        s = jnp.var(v, axis=-1, keepdims=True)
        return (v - m) / jnp.sqrt(s + eps)

    def _to_tokens(v):
        B_, C_, H_, W_ = v.shape
        return v.reshape(B_, C_, H_ * W_).transpose(0, 2, 1)

    def _from_tokens(t, like):
        B_, C_, H_, W_ = like.shape
        return t.transpose(0, 2, 1).reshape(B_, C_, H_, W_)
    x = x + _L0_conv_ref(_gn(x))
    x = x + _L1_conv_ref(_gn(x), L1_conv_W1, L1_conv_b1, L1_conv_g1, L1_conv_beta1, L1_conv_W2, L1_conv_b2, L1_conv_g2, L1_conv_beta2, L1_conv_W3, L1_conv_b3)
    return x

_drawn_inputs = setup_inputs


def setup_inputs(seed=0):
    import zlib

    import numpy as np

    out = dict(_drawn_inputs(seed))
    spreads = {'L1_conv_g1': (1.0, 0.2),
     'L1_conv_beta1': (0.0, 0.1),
     'L1_conv_g2': (1.0, 0.2),
     'L1_conv_beta2': (0.0, 0.283)}
    factors = {}
    for name, (base, spread) in spreads.items():
        noise = np.random.default_rng([zlib.crc32(name.encode()), seed]).standard_normal(out[name].shape)
        drawn = base * np.exp(spread * noise) if base else spread * noise
        out[name] = jnp.asarray(drawn.astype(out[name].dtype))
    for name, factor in factors.items():
        out[name] = (out[name] * factor).astype(out[name].dtype)
    return out
```

```python
from contextlib import ExitStack

import numpy as np
import concourse.bass as bass
from concourse import mybir

F32, F16 = mybir.dt.float32, mybir.dt.float16
ACT = mybir.ActivationFunctionType
ALU = mybir.AluOpType
AX = mybir.AxisListType

B, C, HW = 16, 192, 56 * 56
CA, CC = 128, 64
PAIRS = B // 2
U = 7
UT = HW // U
K = 4
TT = UT // K
GROUP = C // 32
BLK = HW
SLOT = 3 * BLK
NX = 3
W_SCALE = 64.0
GN_EPS, LN_EPS = 1e-5, 1e-6
BND, BNA = 6, 2
TM_BANKS = 3
AA, CIA, CJA, AIC, AJC, CCB = range(6)
H_STEPS = {2: (0, 1), 3: (2, 3), 4: (4, 5), 5: (6,)}
STAT_STEPS = {0: (0, 1, 2, 3), 1: (4, 5, 6)}
GN1_STEP, GN2_STEP = 1, 5


def build(nc, x, w1t, w2t, w3t, b1, b2, b3, g1, be1, g2, be2, consts, out):
    ctx = ExitStack()
    with ctx:
        def sb(name, shape, dt):
            return ctx.enter_context(nc.sbuf_tensor(name, shape, dt))

        def sem(name):
            return ctx.enter_context(nc.semaphore(name))

        X = sb("X", [128, NX * SLOT], F32)
        xs_hi = sb("xs_hi", [128, 2, 3, UT], F16)
        xs_lo = sb("xs_lo", [128, 2, 3, UT], F16)
        x1n = sb("x1n", [128, 3, UT], F32)
        x1_hi = sb("x1_hi", [128, 2, 3, UT], F16)
        x1_lo = sb("x1_lo", [128, 2, 3, UT], F16)
        z = [sb(f"z{n}", [TT, K, 2 * C], F32) for n in (1, 2)]
        ge = [sb(f"ge{n}", [128, 3, UT], F32) for n in (1, 2)]
        ge_hi = [sb(f"ge_hi{n}", [128, 2, 3, UT], F16) for n in (1, 2)]
        ge_lo = [sb(f"ge_lo{n}", [128, 2, 3, UT], F16) for n in (1, 2)]
        w_hi = [sb(f"w_hi{n}", [128, 4, C], F16) for n in (1, 2)]
        w_lo = [sb(f"w_lo{n}", [128, 4, C], F16) for n in (1, 2)]
        w3_hi = sb("w3_hi", [128, 6, 128], F16)
        w3_lo = sb("w3_lo", [128, 6, 128], F16)
        h16 = sb("h16", [128, 6, 128], F16)
        cst = sb("cst", [128, 13 * 128 + 1], F32)
        group_mean = cst[:, 0:768].rearrange("p (b m) -> p b m", b=6)
        h32 = cst[:, 768:1536].rearrange("p (b m) -> p b m", b=6)
        ident = cst[:, 1536:1664]
        row1 = cst[:, 1664:1665]
        bias_rows = [sb(f"bias{n}", [128, 2, C], F16) for n in (1, 2)]
        ones = sb("ones", [128, TT], F16)
        neg_half = sb("neg_half", [128, 4], F32)
        par = sb("par", [128, 11], F32)
        ssq = [sb(f"ssq{n}", [TT, K, 2], F32) for n in (1, 2)]
        ve = [sb(f"ve{n}", [TT, K, 2], F32) for n in (1, 2)]
        rs = [sb(f"rs{n}", [TT, K, 2], F32) for n in (1, 2)]
        bn = [sb(f"bn{n}", [128, 3, U, BND], F32) for n in (1, 2)]
        gst = sb("gst", [128, 2, 3], F32)
        gsq = sb("gsq", [128, 3], F32)
        gmu = sb("gmu", [128, 3, 2], F32)
        gvar = sb("gvar", [128, 3], F32)
        gscale = [sb(f"gscale{n}", [128, 3], F32) for n in (1, 2)]
        gshift = [sb(f"gshift{n}", [128, 3], F32) for n in (1, 2)]
        h_bias = sb("h_bias", [128, 3], F32)
        wsum = sb("wsum", [128, 8], F32)

        tm = [ctx.enter_context(nc.psum_tensor(f"tm{i}", [TT, 2, C], F32)) for i in range(TM_BANKS)]
        tp = ctx.enter_context(nc.psum_tensor("tp", [128, 3, 512], F32))
        hp = ctx.enter_context(nc.psum_tensor("hp", [128, 512], F32))
        lp = ctx.enter_context(nc.psum_tensor("lp", [128, 512], F32))

        s_zero = sem("staging_zeroed")
        s_wload = sem("weights_loaded")
        s_cload = sem("constants_loaded")
        s_prep = sem("weights_ready")
        s_chain = sem("dve_chain")
        s_load = sem("x_loaded")
        s_xs_hi, s_xs_lo = sem("xs_hi_ready"), sem("xs_lo_ready")
        s_h = sem("h_out_ready")
        s_res = sem("residual_done")
        s_bn = [sem("bn_stats_x"), sem("bn_stats_x1")]
        s_gst = sem("gn_stats_ready")
        s_gred = sem("gn_reduced")
        s_gread = sem("gn_psum_read")
        s_gvar = sem("gn_var_ready")
        s_grs = sem("gn_rstd_ready")
        s_gn = [sem("gn1_ready"), sem("gn2_ready")]
        s_x1_hi, s_x1_lo = sem("x1_hi_ready"), sem("x1_lo_ready")
        s_mm = [sem(f"mm{n}_done") for n in (1, 2)]
        s_ssq = [sem(f"ssq{n}_ready") for n in (1, 2)]
        s_ve = [sem(f"ve{n}_ready") for n in (1, 2)]
        s_rs = [sem(f"rstd{n}_ready") for n in (1, 2)]
        s_z = [sem(f"z{n}_ready") for n in (1, 2)]
        s_tp = [sem(f"transposed{n}") for n in (1, 2)]
        s_ge = [sem(f"gelu{n}_done") for n in (1, 2)]
        s_ge_hi = [sem(f"gelu_hi{n}_ready") for n in (1, 2)]
        s_ge_lo = [sem(f"gelu_lo{n}_ready") for n in (1, 2)]
        s_l3 = sem("l3_out_ready")
        s_fin = sem("out_ready")
        s_store = sem("stored")

        s_passed = {e.engine: sem(f"waits_passed_{n}")
                    for n, e in enumerate((nc.scalar, nc.vector, nc.gpsimd))}

        def later(value):
            return not isinstance(value, int) or value > 0

        def passed(eng, value):
            if not isinstance(value, int):
                eng.sem_inc(s_passed[eng.engine], 1)

        def xcols(p, b, u):
            return X[:, bass.ds((p % NX) * SLOT + b * BLK + u * UT, UT)]

        def freed(g, u):
            return g + 1 - {0: 1, 1: 3}.get(u, 2)

        def prev(p, u, d):
            return U * p + u - d, (u - d) % U

        def exists(p, u, layer):
            if not isinstance(p, int):
                return True
            return 0 <= U * p + u + 1 - layer < U * PAIRS

        def tm_bank(u, n, k):
            return (8 * u + 4 * n + k) % TM_BANKS

        def tm_before(p, u, n, k):
            pos = 8 * u + 4 * n + k
            d = {0: 2, 1: 2, 2: 5}.get(pos, 3)
            while True:
                at = pos - d
                up, off = at // 8, at % 8
                g = U * p + up
                n0, k0 = off // 4, off % 4
                if isinstance(g, int):
                    if g < 0:
                        return None
                    if not 0 <= g - n0 < U * PAIRS:
                        d += 3 if at >= 3 else {0: 2, 1: 2, 2: 5}.get(at, 3)
                        continue
                return s_z[n0], K * (g - n0) + k0 + 1

        stage = X[:, 2 * SLOT:3 * SLOT]
        wst = [stage[:, n * 4 * C:(n + 1) * 4 * C].rearrange("p (b o) -> p b o", b=4) for n in (0, 1)]
        w3st = stage[:, 8 * C:8 * C + 768].rearrange("p (b o) -> p b o", b=6)
        bst = stage[:, 8 * C + 768:12 * C + 768].rearrange("p (n i o) -> p n i o", n=2, i=2)
        ZEROED = 12 * C + 768

        block = ctx.enter_context(nc.Block())

        @block.sync
        def _(sp):
            def load(p):
                sp.dma_start(X[:, bass.ds((p % NX) * SLOT, 2 * BLK)].rearrange("c (i t) -> c i t", i=2),
                             x[bass.ds(2 * p, 2), 0:CA, :].rearrange("i c t -> c i t")).then_inc(s_load, 16)
                for i in range(2):
                    sp.dma_start(X[i * CC:(i + 1) * CC, bass.ds((p % NX) * SLOT + 2 * BLK, BLK)],
                                 x[bass.ds(2 * p + i, 1), CA:C, :].rearrange("i c t -> c (i t)")).then_inc(s_load, 16)

            def store(p, u):
                sp.wait_ge(s_fin, 3 * (U * p + u + 1))
                t0 = u * UT
                sp.dma_start(out[bass.ds(2 * p, 2), 0:CA, t0:t0 + UT].rearrange("i c t -> c i t"),
                             X[:, bass.ds((p % NX) * SLOT, 2 * BLK)].rearrange("c (i t) -> c i t", i=2)[:, :, t0:t0 + UT]
                             ).then_inc(s_store, 16)
                for i in range(2):
                    sp.dma_start(out[bass.ds(2 * p + i, 1), CA:C, t0:t0 + UT].rearrange("i c t -> c (i t)"),
                                 X[i * CC:(i + 1) * CC, bass.ds((p % NX) * SLOT + 2 * BLK + t0, UT)]
                                 ).then_inc(s_store, 16)

            load(0)
            sp.dma_start(cst[:, :], consts).then_inc(s_cload, 16)
            for col, (v, lo, hi) in enumerate([(g1, 0, CA), (g1, CA, C), (be1, 0, CA), (be1, CA, C),
                                               (g2, 0, CA), (g2, CA, C), (be2, 0, CA), (be2, CA, C),
                                               (b3, 0, CA), (b3, 0, CA), (b3, CA, C)]):
                n = hi - lo
                for r in range(0, 128, n):
                    sp.dma_start(par[r:r + n, col:col + 1], v[lo:hi].rearrange("(c a) -> c a", a=1)).then_inc(s_cload, 16)
            sp.wait_ge(s_zero, 1)
            for n, wt in enumerate((w1t, w2t)):
                sp.dma_start(wst[n][:, 0, :], wt[0:CA, :]).then_inc(s_wload, 16)
                sp.dma_start(wst[n][0:CC, 1, :], wt[CA:C, :]).then_inc(s_wload, 16)
                for blk, rows, src in ((2, slice(CC, 128), wt[CA:C]), (3, slice(0, 128), wt[0:CA])):
                    sp.dma_start(wst[n][rows, blk, 0:CC], src[:, CA:C]).then_inc(s_wload, 16)
                    sp.dma_start(wst[n][rows, blk, CC:C], src[:, 0:CA]).then_inc(s_wload, 16)
            sp.dma_start(w3st[:, AA, :], w3t[0:CA, 0:CA]).then_inc(s_wload, 16)
            sp.dma_start(w3st[0:CC, CIA, :], w3t[CA:C, 0:CA]).then_inc(s_wload, 16)
            sp.dma_start(w3st[CC:128, CJA, :], w3t[CA:C, 0:CA]).then_inc(s_wload, 16)
            sp.dma_start(w3st[:, AIC, 0:CC], w3t[0:CA, CA:C]).then_inc(s_wload, 16)
            sp.dma_start(w3st[:, AJC, CC:128], w3t[0:CA, CA:C]).then_inc(s_wload, 16)
            sp.dma_start(w3st[0:CC, CCB, 0:CC], w3t[CA:C, CA:C]).then_inc(s_wload, 16)
            sp.dma_start(w3st[CC:128, CCB, CC:128], w3t[CA:C, CA:C]).then_inc(s_wload, 16)
            for n, bv in enumerate((b1, b2)):
                bv = bv.rearrange("(a o) -> a o", a=1)
                for r in range(2):
                    sp.dma_start(bst[r:r + 1, n, 0, :], bv).then_inc(s_wload, 16)
                    sp.dma_start(bst[r:r + 1, n, 1, 0:CC], bv[:, CA:C]).then_inc(s_wload, 16)
                    sp.dma_start(bst[r:r + 1, n, 1, CC:C], bv[:, 0:CA]).then_inc(s_wload, 16)
            sp.wait_ge(s_load, 48)
            load(1)
            sp.wait_ge(s_prep, 1)
            sp.wait_ge(s_load, 96)
            load(2)

            def stores(p):
                for u in range(U):
                    store(p, u)

            with sp.Fori(0, PAIRS - NX) as p:
                stores(p)
                sp.wait_ge(s_store, 48 * U * (p + 1))
                load(p + NX)
            with sp.Fori(PAIRS - NX, PAIRS) as p:
                stores(p)
            sp.wait_ge(s_store, 48 * U * PAIRS)

        @block.tensor
        def _(pe):
            def gn_reduce(j):
                pe.wait_ge(s_gst, j + 1)
                for b, terms in enumerate((((AA, 0), (CIA, 2)), ((AA, 1), (CJA, 2)), ((AIC, 0), (AJC, 1), (CCB, 2)))):
                    for i, (m, src) in enumerate(terms):
                        last = nc.tensor.matmul(hp[:, 2 * b:2 * b + 2], group_mean[:, m, :], gst[:, :, src],
                                                start=(i == 0), stop=(i == len(terms) - 1))
                last.then_inc(s_gred, 1)

            def gn1(q):
                if later(3 * q):
                    pe.wait_ge(s_gread, 3 * q)
                gn_reduce(2 * q)
                pe.wait_ge(s_gread, 3 * q + 1)
                pe.wait_ge(s_gn[0], 2 * q + 1)
                for b, terms in enumerate((((AA, 0), (CIA, 2)), ((AA, 1), (CJA, 2)), ((AIC, 0), (AJC, 1), (CCB, 2)))):
                    for i, (m, src) in enumerate(terms):
                        last = nc.tensor.matmul(hp[:, b:b + 1], h32[:, m, :], gshift[0][:, src:src + 1],
                                                start=(i == 0), stop=(i == len(terms) - 1))
                last.then_inc(s_gred, 1)

            def gn2(q):
                pe.wait_ge(s_res, 21 * (q + 1))
                gn_reduce(2 * q + 1)

            def h_out(q, c, b):
                a = U * q + c
                if b == 0:
                    pe.wait_ge(s_xs_lo, a + 1)
                if c == 0 and b == 0:
                    pe.wait_ge(s_gread, 3 * q + 2)
                else:
                    if later(3 * a + b):
                        pe.wait_ge(s_res, 3 * a + b)
                hi, lo = xs_hi[:, c % 2], xs_lo[:, c % 2]
                if b < 2:
                    terms = [(AA, b, 0, 128), ((CIA, CJA)[b], 2, 0, 128)]
                else:
                    terms = [(CCB, 2, 0, 128), (AIC, 0, 0, 64), (AJC, 1, 64, 128)]
                n = 0
                for m, src, lo_p, hi_p in terms:
                    for part in (hi, lo):
                        last = nc.tensor.matmul(hp[lo_p:hi_p, 0:UT], h16[:, m, lo_p:hi_p], part[:, src, :],
                                                start=(n == 0), stop=(m in ((CIA, CJA) if b < 2 else (AIC, AJC)) and part is lo),
                                                skip_group_check=True)
                        n += 1
                last.then_inc(s_h, 1)

            def group(p, u, n, k):
                g, un = prev(p, u, n)
                if k == 0:
                    pe.wait_ge((s_x1_lo, s_ge_lo[0])[n], g + 1)
                before = tm_before(p, u, n, k)
                if before:
                    pe.wait_ge(*before)
                dst = tm[tm_bank(u, n, k)]
                hi, lo = ((x1_hi, x1_lo), (ge_hi[0], ge_lo[0]))[n]
                cols = slice(k * TT, (k + 1) * TT)
                nc.tensor.matmul(dst[:, :, :], ones[:, :], bias_rows[n][:, :, :], start=True, stop=False,
                                 skip_group_check=True)
                for act, w in ((hi, w_hi[n]), (hi, w_lo[n]), (lo, w_hi[n])):
                    nc.tensor.matmul(dst[:, :, :], act[:, un % 2, 2, cols], w[:, 1:3, :], start=False, stop=False,
                                     skip_group_check=True)
                for i in range(2):
                    for r, (act, w) in enumerate(((hi, w_hi[n]), (hi, w_lo[n]), (lo, w_hi[n]))):
                        last = nc.tensor.matmul(dst[:, i, :], act[:, un % 2, i, cols], w[:, 3 * i, :], start=False,
                                                stop=(r == 2), skip_group_check=True)
                last.then_inc(s_mm[n], 1)

            def transposes(p, u, n, k):
                g, _ = prev(p, u, n)
                if k == 0:
                    if n == 0:
                        if later(2 * (g - 1)):
                            pe.wait_ge(s_ge[1], 2 * (g - 1))
                    else:
                        pe.wait_ge(s_ge[0], 2 * min(g + 2, U * PAIRS) if isinstance(g, int) else 2 * (g + 2))
                pe.wait_ge(s_z[n], K * g + k + 1)
                cols = slice(k * TT, (k + 1) * TT)
                for blk, at in ((0, 0), (1, C + CC), (2, CA)):
                    last = nc.tensor.transpose(tp[:, blk, cols], z[n][:, k, at:at + 128], ident[0:TT, 0:TT])
                if k == K - 1:
                    last.then_inc(s_tp[n], 1)

            def l3_out(p, u, b):
                g, u3 = prev(p, u, 2)
                if b == 0:
                    pe.wait_ge(s_ge_lo[1], g + 1)
                if later(3 * g + b):
                    pe.wait_ge(s_fin, 3 * g + b)
                hi, lo = ge_hi[1][:, u3 % 2], ge_lo[1][:, u3 % 2]
                if b < 2:
                    terms = [(AA, b, 0, 128), ((CIA, CJA)[b], 2, 0, 128)]
                else:
                    terms = [(CCB, 2, 0, 128), (AIC, 0, 0, 64), (AJC, 1, 64, 128)]
                ends = (CIA, CJA) if b < 2 else (AIC, AJC)
                n = 0
                for m, src, lo_p, hi_p in terms:
                    for r, (w, act) in enumerate(((w3_hi, hi), (w3_hi, lo), (w3_lo, hi))):
                        last = nc.tensor.matmul(lp[lo_p:hi_p, 0:UT], w[:, m, lo_p:hi_p], act[:, src, :],
                                                start=(n == 0), stop=(m in ends and r == 2), skip_group_check=True)
                        n += 1
                last.then_inc(s_l3, 1)

            def step(p, u, next_pair):
                hs = H_STEPS.get(u, ()) if next_pair else ()
                q = p + 1
                h0 = hs[0] if hs else None
                h1 = hs[1] if len(hs) > 1 else None
                for n in range(2):
                    have = exists(p, u, n + 1)
                    hc = (h0, h1)[n]
                    have3 = n == 1 and exists(p, u, 3)
                    for k in range(K + 2):
                        if have and k < K:
                            group(p, u, n, k)
                        if k >= 2:
                            if have:
                                transposes(p, u, n, k - 2)
                            if k >= 3:
                                if hc is not None:
                                    h_out(q, hc, k - 3)
                                if have3:
                                    l3_out(p, u, k - 3)
                if next_pair and u == GN1_STEP:
                    gn1(q)
                if next_pair and u == GN2_STEP:
                    gn2(q)

            pe.wait_ge(s_cload, 16 * CLOADS)
            pe.wait_ge(s_prep, 1)
            gn1(0)
            for c in range(U):
                for b in range(3):
                    h_out(0, c, b)
            gn2(0)
            run(pe, step)

        @block.scalar
        def _(act):
            def scaled_hi(q, c):
                a = U * q + c
                if c == 0:
                    act.wait_ge(s_gn[0], 2 * q + 2)
                if later(3 * freed(a, c)):
                    act.wait_ge(s_h, 3 * freed(a, c))
                    passed(act, 3 * freed(a, c))
                for b in range(3):
                    last = nc.scalar.activation(xs_hi[:, c % 2, b, :], xcols(q, b, c), ACT.Copy,
                                                scale=gscale[0][:, b:b + 1])
                last.then_inc(s_xs_hi, 1)

            def split_x1(p, u):
                g = U * p + u
                if u == 0:
                    act.wait_ge(s_gn[1], p + 1)
                if later(g):
                    act.wait_ge(s_x1_lo, g)
                    passed(act, g)
                for b in range(3):
                    nc.scalar.activation(x1n[:, b, :], xcols(p, b, u), ACT.Identity,
                                         bias=gshift[1][:, b:b + 1], scale=gscale[1][:, b:b + 1])
                if later(K * freed(g, u)):
                    act.wait_ge(s_mm[0], K * freed(g, u))
                    passed(act, K * freed(g, u))
                for b in range(3):
                    last = nc.scalar.activation(x1_hi[:, u % 2, b, :], xcols(p, b, u), ACT.Identity,
                                                bias=gshift[1][:, b:b + 1], scale=gscale[1][:, b:b + 1])
                last.then_inc(s_x1_hi, 1)

            def squares(p, u, n, k):
                g, _ = prev(p, u, n)
                act.wait_ge(s_mm[n], K * g + k + 1)
                for i in range(2):
                    last = nc.scalar.activation(z[n][:, k, i * C:(i + 1) * C], tm[tm_bank(u, n, k)][:, i, :], ACT.Square,
                                                accum_out=ssq[n][:, k, i:i + 1])
                last.then_inc(s_ssq[n], 1)

            def gelu(p, u, n):
                g, _ = prev(p, u, n)
                act.wait_ge(s_tp[n], g + 1)
                if later(g):
                    act.wait_ge(s_ge_lo[n], g)
                for blocks, c in ((slice(0, 2), 0), (slice(2, 3), 1)):
                    nc.scalar.activation(ge[n][:, blocks, :], tp[:, blocks, 0:UT], ACT.Gelu,
                                         bias=par[:, 4 * n + 2 + c:4 * n + 3 + c],
                                         scale=par[:, 4 * n + c:4 * n + c + 1]).then_inc(s_ge[n], 1)

            def gelu_hi(g, un, n):
                act.wait_ge(s_ge[n], 2 * (g + 1))
                if later((K, 3)[n] * freed(g, un)):
                    act.wait_ge((s_mm[1], s_l3)[n], (K, 3)[n] * freed(g, un))
                nc.scalar.activation(ge_hi[n][:, un % 2], ge[n][:, :, :], ACT.Copy).then_inc(s_ge_hi[n], 1)

            def step(p, u, next_pair):
                hs = H_STEPS.get(u, ()) if next_pair else ()
                one, two, three = (exists(p, u, n) for n in (1, 2, 3))
                for k in range(K):
                    if one:
                        squares(p, u, 0, k)
                    if k == 1 and three:
                        gelu_hi(*prev(p, u, 2), 1)
                    if k == 2 and len(hs) > 0 and u == min(H_STEPS):
                        scaled_hi(p + 1, hs[0])
                if len(hs) > 1:
                    scaled_hi(p + 1, hs[1])
                if u < U - 1 and one:
                    split_x1(p, u + 1)
                elif next_pair:
                    split_x1(p + 1, 0)
                if one:
                    gelu(p, u, 0)
                for k in range(K):
                    if two:
                        squares(p, u, 1, k)
                    if k == 1 and one:
                        gelu_hi(U * p + u, u, 0)
                if next_pair and u + 1 in H_STEPS and u + 1 != min(H_STEPS):
                    scaled_hi(p + 1, H_STEPS[u + 1][0])
                if two:
                    gelu(p, u, 1)

            act.wait_ge(s_cload, 16 * CLOADS)
            for c in range(U):
                scaled_hi(0, c)
            split_x1(0, 0)
            run(act, step)

        @block.gpsimd
        def _(pool):
            def gn(q, n):
                pool.wait_ge(s_gvar, 2 * q + n + 1)
                nc.gpsimd.tensor_tensor(gscale[n][:, :], gvar[:, :], neg_half[:, 0:3], ALU.pow).then_inc(s_grs, 1)

            def rstd(p, u, n, k):
                g, _ = prev(p, u, n)
                pool.wait_ge(s_ssq[n], K * g + k + 1)
                passed(pool, K * g + k + 1)
                nc.gpsimd.tensor_scalar(ve[n][:, k, :], ssq[n][:, k, :], 1.0 / C, LN_EPS * W_SCALE ** 2,
                                        ALU.mult, ALU.add).then_inc(s_ve[n], 1)
                pool.wait_ge(s_ve[n], K * g + k + 1)
                nc.gpsimd.tensor_tensor(rs[n][:, k, :], ve[n][:, k, :], neg_half[0:TT, 0:2],
                                        ALU.pow).then_inc(s_rs[n], 1)

            def gelu_lo(g, un, n):
                pool.wait_ge(s_ge_hi[n], g + 1)
                for b in range(3):
                    last = nc.gpsimd.tensor_tensor(ge_lo[n][:, un % 2, b, :], ge[n][:, b, :],
                                                   ge_hi[n][:, un % 2, b, :], ALU.subtract)
                last.then_inc(s_ge_lo[n], 1)

            def step(p, u, next_pair):
                one, two, three = (exists(p, u, n) for n in (1, 2, 3))
                if one:
                    for k in range(K):
                        rstd(p, u, 0, k)
                if three:
                    gelu_lo(*prev(p, u, 2), 1)
                if two:
                    for k in range(K):
                        rstd(p, u, 1, k)
                if one:
                    gelu_lo(U * p + u, u, 0)
                if next_pair and u == GN1_STEP:
                    gn(p + 1, 0)
                if next_pair and u == GN2_STEP:
                    gn(p + 1, 1)

            pool.wait_ge(s_prep, 1)
            gn(0, 0)
            gn(0, 1)
            run(pool, step)

        @block.vector
        def _(dve):
            links = {"at": 0}

            def link(ins):
                links["at"] += 1
                ins.then_inc(s_chain, 1)
                dve.wait_ge(s_chain, links["at"])

            PER = 16

            def prepare():
                link(nc.vector.memset(stage[:, 0:ZEROED], 0.0))
                nc.vector.memset(ones[:, :], 1.0)
                nc.vector.memset(neg_half[:, :], -0.5).then_inc(s_zero, 1)
                dve.wait_ge(s_cload, 16 * CLOADS)
                nc.vector.tensor_copy(h16[:, :, :], h32)

            def weights():
                dve.wait_ge(s_wload, 16 * WLOADS)
                for n in range(2):
                    link(nc.vector.reduce_sum(wsum[:, 0:4], wst[n], axis=AX.X))
                    link(nc.vector.tensor_scalar(wsum[:, 0:4], wsum[:, 0:4], 1.0 / C, None, ALU.mult))
                    link(nc.vector.tensor_tensor(wst[n], wst[n], wsum[:, 0:4].unsqueeze(2).to_broadcast([128, 4, C]),
                                                 ALU.subtract))
                    link(nc.vector.tensor_scalar(wst[n], wst[n], W_SCALE, None, ALU.mult))
                    link(nc.vector.tensor_copy(w_hi[n][:, :, :], wst[n]))
                    nc.vector.tensor_tensor(w_lo[n][:, :, :], wst[n], w_hi[n][:, :, :], ALU.subtract)
                link(nc.vector.reduce_sum(wsum[:, 4:6], bst[:, :, 0, :], axis=AX.X))
                link(nc.vector.tensor_scalar(wsum[:, 4:6], wsum[:, 4:6], -1.0 / C, None, ALU.mult))
                for n in range(2):
                    link(nc.vector.tensor_scalar(bst[:, n], bst[:, n], wsum[:, 4 + n:5 + n], W_SCALE, ALU.add, ALU.mult))
                    link(nc.vector.tensor_copy(bias_rows[n][:, :, :], bst[:, n]))
                    link(nc.vector.scalar_tensor_tensor(out=wst[0][:, 2 * n:2 * n + 2, :], in0=bias_rows[n][:, :, :],
                                                        scalar=row1, in1=bst[:, n], op0=ALU.mult, op1=ALU.subtract))
                    last = nc.vector.tensor_scalar(bias_rows[n][:, :, :], wst[0][:, 2 * n:2 * n + 2, :], -1.0, None, ALU.mult)
                link(last)
                link(nc.vector.tensor_scalar(w3st, w3st, W_SCALE, None, ALU.mult))
                link(nc.vector.tensor_copy(w3_hi[:, :, :], w3st))
                nc.vector.tensor_tensor(w3_lo[:, :, :], w3st, w3_hi[:, :, :], ALU.subtract).then_inc(s_prep, 1)

            def stats_x(q, cs):
                if cs[0] == 0:
                    dve.wait_ge(s_load, 48 * (q + 1))
                    passed(dve, 48 * (q + 1))
                for c in cs:
                    for b in range(3):
                        last = nc.vector.bn_stats(bn[0][:, b, c, :], xcols(q, b, c))
                    last.then_inc(s_bn[0], 1)

            def scaled_lo(q, c):
                a = U * q + c
                dve.wait_ge(s_xs_hi, a + 1)
                for b in range(3):
                    last = nc.vector.scalar_tensor_tensor(out=xs_lo[:, c % 2, b, :], in0=xcols(q, b, c),
                                                          scalar=gscale[0][:, b:b + 1], in1=xs_hi[:, c % 2, b, :],
                                                          op0=ALU.mult, op1=ALU.subtract)
                last.then_inc(s_xs_lo, 1)

            def residual(q, c, b):
                r = 3 * (U * q + c) + b + 1
                dve.wait_ge(s_h, r)
                nc.vector.scalar_tensor_tensor(out=xcols(q, b, c), in0=hp[:, 0:UT], scalar=h_bias[:, b:b + 1],
                                               in1=xcols(q, b, c), op0=ALU.add, op1=ALU.add).then_inc(s_res, 1)

            def stats_x1(q, c):
                dve.wait_ge(s_res, 3 * (U * q + c) + 3)
                passed(dve, 3 * (U * q + c) + 3)
                for b in range(3):
                    last = nc.vector.bn_stats(bn[1][:, b, c, :], xcols(q, b, c))
                last.then_inc(s_bn[1], 1)

            def chain(q, n):
                at = [0]

                def do(ins):
                    at[0] += 1
                    ins.then_inc(s_chain, 1)
                    dve.wait_ge(s_chain, BASE + 2 * PER * q + PER * n + at[0])

                def fill():
                    dve.sem_inc(s_chain, PER - at[0]) if PER > at[0] else None

                return do, fill

            def groupnorm(q, n):
                do, fill = chain(q, n)
                j = 2 * q + n
                dve.wait_ge(s_bn[n], U * (q + 1))
                passed(dve, U * (q + 1))
                for b in range(3):
                    last = nc.vector.bn_aggr(gst[:, :, b], bn[n][:, b, :, :].rearrange("p u s -> p (u s)"))
                do(last)
                if n == 1:
                    do(nc.vector.tensor_tensor(gst[:, 0, :], gst[:, 0, :], par[:, 8:11], ALU.subtract))
                do(nc.vector.tensor_tensor(gsq[:, :], gst[:, 0, :], gst[:, 0, :], ALU.mult))
                nc.vector.tensor_tensor(gst[:, 1, :], gst[:, 1, :], gsq[:, :], ALU.add).then_inc(s_gst, 1)
                gr = 3 * q + (0, 2)[n]
                dve.wait_ge(s_gred, gr + 1)
                nc.vector.tensor_copy(gmu[:, :, :], hp[:, 0:6].rearrange("p (b s) -> p b s", b=3)).then_inc(s_gread, 1)
                dve.wait_ge(s_gread, gr + 1)
                do(nc.vector.tensor_tensor(gsq[:, :], gmu[:, :, 0], gmu[:, :, 0], ALU.mult))
                do(nc.vector.tensor_tensor(gvar[:, :], gmu[:, :, 1], gsq[:, :], ALU.subtract))
                do(nc.vector.tensor_scalar(gvar[:, :], gvar[:, :], 0.0, GN_EPS, ALU.max, ALU.add))
                dve.sem_inc(s_gvar, 1)
                dve.wait_ge(s_grs, j + 1)
                do(nc.vector.scalar_tensor_tensor(out=gshift[n][:, :], in0=gmu[:, :, 0], scalar=-1.0,
                                                  in1=gscale[n][:, :], op0=ALU.mult, op1=ALU.mult))
                if n == 0:
                    dve.sem_inc(s_gn[0], 1)
                    dve.wait_ge(s_gred, gr + 2)
                    nc.vector.tensor_tensor(h_bias[:, :], hp[:, 0:3], par[:, 8:11], ALU.add).then_inc(s_gread, 1)
                    dve.wait_ge(s_gread, gr + 2)
                    dve.sem_inc(s_gn[0], 1)
                else:
                    do(nc.vector.tensor_tensor(gsq[:, :], gscale[1][:, :], par[:, 8:11], ALU.mult))
                    do(nc.vector.tensor_tensor(gshift[1][:, :], gshift[1][:, :], gsq[:, :], ALU.subtract))
                    dve.sem_inc(s_gn[1], 1)
                fill()

            def x1_split_lo(p, u):
                g = U * p + u
                dve.wait_ge(s_x1_hi, g + 1)
                nc.vector.tensor_tensor(x1_lo[:, u % 2], x1n[:, :, :], x1_hi[:, u % 2], ALU.subtract).then_inc(s_x1_lo, 1)

            def normalise(p, u, n, k):
                g, _ = prev(p, u, n)
                dve.wait_ge(s_rs[n], K * g + k + 1)
                nc.vector.tensor_tensor(z[n][:, k], tm[tm_bank(u, n, k)][:, :, :],
                                        rs[n][:, k, :].unsqueeze(2).to_broadcast([TT, 2, C]),
                                        ALU.mult).then_inc(s_z[n], 1)

            def final(p, u, b):
                g, u3 = prev(p, u, 2)
                pp = p if u >= 2 else p - 1
                dve.wait_ge(s_l3, 3 * g + b + 1)
                nc.vector.scalar_tensor_tensor(out=xcols(pp, b, u3), in0=lp[:, 0:UT], scalar=1.0 / W_SCALE,
                                               in1=xcols(pp, b, u3), op0=ALU.mult, op1=ALU.add).then_inc(s_fin, 1)

            def step(p, u, next_pair):
                hs = H_STEPS.get(u, ()) if next_pair else ()
                one, two, three = (exists(p, u, n) for n in (1, 2, 3))
                q = p + 1
                if next_pair and u in STAT_STEPS:
                    stats_x(q, STAT_STEPS[u][:2])
                for k in range(K):
                    if one:
                        normalise(p, u, 0, k)
                    if k == 2 and hs and u == min(H_STEPS):
                        scaled_lo(q, hs[0])
                if len(hs) > 1:
                    scaled_lo(q, hs[1])
                if hs:
                    for b in range(3):
                        residual(q, hs[0], b)
                    stats_x1(q, hs[0])
                if next_pair and u in STAT_STEPS:
                    stats_x(q, STAT_STEPS[u][2:]) if len(STAT_STEPS[u]) > 2 else None
                if u < U - 1 and one:
                    x1_split_lo(p, u + 1)
                elif next_pair:
                    x1_split_lo(q, 0)
                if two:
                    for k in range(K):
                        normalise(p, u, 1, k)
                for b in range(3):
                    if len(hs) > 1:
                        residual(q, hs[1], b)
                    if three:
                        final(p, u, b)
                if len(hs) > 1:
                    stats_x1(q, hs[1])
                if next_pair and u + 1 in H_STEPS and u + 1 != min(H_STEPS):
                    scaled_lo(q, H_STEPS[u + 1][0])
                if next_pair and u == GN1_STEP:
                    groupnorm(q, 0)
                if next_pair and u == GN2_STEP:
                    groupnorm(q, 1)

            prepare()
            weights()
            BASE = links["at"]
            stats_x(0, tuple(range(U)))
            groupnorm(0, 0)
            for c in range(U):
                scaled_lo(0, c)
                for b in range(3):
                    residual(0, c, b)
                stats_x1(0, c)
            groupnorm(0, 1)
            x1_split_lo(0, 0)
            run(dve, step)


CLOADS = 1 + 5 + 5 * 2 + 1
WLOADS = 2 * 6 + 7 + 2 * 2 * 3


def run(eng, step):
    for u in range(U):
        step(0, u, True)
    with eng.Fori(1, PAIRS - 1) as p:
        for u in range(U):
            step(p, u, True)
    for u in range(U):
        step(PAIRS - 1, u, False)
    step(PAIRS, 0, False)
    step(PAIRS, 1, False)


def blocks6(m):
    r = np.zeros((128, 6, 128), np.float32)
    r[:, AA] = m[:CA, :CA]
    r[:CC, CIA] = m[CA:, :CA]
    r[CC:, CJA] = m[CA:, :CA]
    r[:, AIC, :CC] = m[:CA, CA:]
    r[:, AJC, CC:] = m[:CA, CA:]
    r[:CC, CCB, :CC] = m[CA:, CA:]
    r[CC:, CCB, CC:] = m[CA:, CA:]
    return r.reshape(128, 768)


def constants():
    had = np.array([[1.0]], np.float32)
    while had.shape[0] < 256:
        had = np.block([[had, had], [had, -had]])
    had = (had / 16.0)[:C, :C].astype(np.float32)
    ch = np.arange(C)
    grp = (ch[:, None] // GROUP == ch[None, :] // GROUP).astype(np.float32) / np.float32(GROUP)
    unit = np.zeros((128, 1), np.float32)
    unit[1] = 1.0
    return np.concatenate([blocks6(grp), blocks6(had), np.eye(128, dtype=np.float32), unit], axis=1)


def kernel(x, L1_conv_W1, L1_conv_b1, L1_conv_g1, L1_conv_beta1, L1_conv_W2, L1_conv_b2,
           L1_conv_g2, L1_conv_beta2, L1_conv_W3, L1_conv_b3):
    import concourse.bacc as bacc
    from concourse.bass_utils import run_bass_kernel_spmd

    x = np.asarray(x)
    arrays = {
        "x": np.ascontiguousarray(x.reshape(B, C, HW)),
        "w1t": np.ascontiguousarray(np.asarray(L1_conv_W1).T),
        "w2t": np.ascontiguousarray(np.asarray(L1_conv_W2).T),
        "w3t": np.ascontiguousarray(np.asarray(L1_conv_W3).T),
        "b1": np.asarray(L1_conv_b1), "b2": np.asarray(L1_conv_b2), "b3": np.asarray(L1_conv_b3),
        "g1": np.asarray(L1_conv_g1), "be1": np.asarray(L1_conv_beta1),
        "g2": np.asarray(L1_conv_g2), "be2": np.asarray(L1_conv_beta2),
        "consts": constants(),
    }
    nc = bacc.Bacc("TRN2", target_bir_lowering=False, num_devices=1)
    args = [nc.dram_tensor(n, a.shape, mybir.dt.from_np(a.dtype), kind="ExternalInput").ap()
            for n, a in arrays.items()]
    out = nc.dram_tensor("out", (B, C, HW), F32, kind="ExternalOutput").ap()
    build(nc, *args, out)
    r = run_bass_kernel_spmd(nc, [arrays], core_ids=[0])
    return r.results[0]["out"].reshape(x.shape)
```

```python
from contextlib import ExitStack

import numpy as np
import concourse.bass as bass
from concourse import mybir

F32, F16 = mybir.dt.float32, mybir.dt.float16
ACT = mybir.ActivationFunctionType
ALU = mybir.AluOpType
AX = mybir.AxisListType

B, C, HW = 16, 192, 56 * 56
CA, CC = 128, 64
PAIRS = B // 2
U = 7
UT = HW // U
K = 4
TT = UT // K
GROUP = C // 32
BLK = HW
SLOT = 3 * BLK
NX = 3
W_SCALE = 64.0
GN_EPS, LN_EPS = 1e-5, 1e-6
BND, BNA = 6, 2
TM_BANKS = 3
AA, CIA, CJA, AIC, AJC, CCB = range(6)
TW = C + 2
GREADS = 4
LOAD_PARTS = ((0, 1, 2), (3, 4, 5), (6,))


def plan(h_at, stats, gn):
    work = {(u, n): {} for u in range(U) for n in range(2)}

    def put(kind, at, dq, what, back=0):
        at = 2 * at[0] + at[1] - back
        if at < 0:
            at, dq = at + 2 * U, dq + 1
        work[at // 2, at % 2][kind] = dq, what

    for c, at in enumerate(h_at):
        put("h", at, 1, c)
        if c > 0:
            put("hi", h_at[c - 1], 1, c)
        else:
            put("hi", at, 1, 0, back=1)
        put("lo", at, 1, c, back=1)
        put("stats_x1" if c == U - 1 else "stats_x1_before", at, 1, c, back=0 if c == U - 1 else -1)
    for at, (dq, units) in stats.items():
        put("stats_x", at, dq, units)
    for at, (dq, n) in gn.items():
        put("gn", at, dq, n)
        put("gn_stats", at, dq, n, back=1)
    return work


LATER_STATS = {(3, 1): (2, (0,)), (4, 0): (2, (1,)), (4, 1): (2, (2,)), (5, 0): (2, (3,)), (5, 1): (2, (4,)),
               (6, 0): (2, (5, 6))}
LATER_GN = {(6, 0): (1, 1), (6, 1): (2, 0)}
PLAN0 = plan([(1, 1), (2, 0), (3, 0), (3, 1), (4, 0), (5, 0), (5, 1)],
             {(0, 0): (1, (0, 1, 2, 3)), (0, 1): (1, (4, 5, 6)), **LATER_STATS}, {(1, 0): (1, 0), **LATER_GN})
PLAN = plan([(0, 0), (1, 0), (2, 0), (3, 0), (4, 0), (5, 0), (5, 1)], LATER_STATS, LATER_GN)
for kind in ("hi", "lo"):
    PLAN0[6, 1][kind] = PLAN[6, 1][kind]


def build(nc, x, weights, biases, params, consts, out):
    ctx = ExitStack()
    with ctx:
        def sb(name, shape, dt):
            return ctx.enter_context(nc.sbuf_tensor(name, shape, dt))

        def sem(name):
            return ctx.enter_context(nc.semaphore(name))

        X = sb("X", [128, NX * SLOT], F32)
        xs_hi = sb("xs_hi", [128, 2, 3, UT], F16)
        xs_lo = sb("xs_lo", [128, 2, 3, UT], F16)
        x1_hi = sb("x1_hi", [128, 2, 3, UT], F16)
        x1_lo = sb("x1_lo", [128, 2, 3, UT], F16)
        z = [sb(f"z{n}", [TT, K, 2 * TW], F32) for n in (1, 2)]
        ge = [sb(f"ge{n}", [128, 3, UT], F32) for n in (1, 2)]
        ge_hi = [sb(f"ge_hi{n}", [128, 2, 3, UT], F16) for n in (1, 2)]
        ge_lo = [sb(f"ge_lo{n}", [128, 2, 3, UT], F16) for n in (1, 2)]
        w_hi = [sb(f"w_hi{n}", [128, 4, C], F16) for n in (1, 2)]
        w_lo = [sb(f"w_lo{n}", [128, 4, C], F16) for n in (1, 2)]
        w32 = sb("w32", [128, 4, C], F32)
        b32 = sb("b32", [2, 2, C], F32)
        b_row = sb("b_row", [2, 2, C], F32)
        w3_hi = sb("w3_hi", [128, 6, 128], F16)
        w3_lo = sb("w3_lo", [128, 6, 128], F16)
        h16 = sb("h16", [128, 6, 128], F16)
        cst = sb("cst", [128, 13 * 128], F32)
        group_mean = cst[:, 0:768].rearrange("p (b m) -> p b m", b=6)
        h32 = cst[:, 768:1536].rearrange("p (b m) -> p b m", b=6)
        ident = cst[:, 1536:1664]
        bias_rows = [sb(f"bias{n}", [128, 2, TW], F16) for n in (1, 2)]
        ones = sb("ones", [128, TT], F16)
        neg_half = sb("neg_half", [128, 4], F32)
        par = sb("par", [128, 12], F32)
        row1 = par[:, 11:12]
        ssq = [sb(f"ssq{n}", [TT, K, 2], F32) for n in (1, 2)]
        rs = [sb(f"rs{n}", [TT, K, 2], F32) for n in (1, 2)]
        bn = [sb(f"bn{n}", [128, 3, U, BND], F32) for n in (1, 2)]
        gst = sb("gst", [128, 2, 3], F32)
        gsq = sb("gsq", [128, 3], F32)
        gmu = sb("gmu", [128, 3, 2], F32)
        gvar = sb("gvar", [128, 3], F32)
        gscale = [sb(f"gscale{n}", [128, 3], F32) for n in (1, 2)]
        gshift = [sb(f"gshift{n}", [128, 3, 2], F32) for n in (1, 2)]
        h_bias = sb("h_bias", [128, 3], F32)
        wsum = sb("wsum", [128, 8], F32)
        bsum = sb("bsum", [2, 2], F32)

        tm = [ctx.enter_context(nc.psum_tensor(f"tm{i}", [TT, 2, TW], F32)) for i in range(TM_BANKS)]
        tp = ctx.enter_context(nc.psum_tensor("tp", [128, 3, 512], F32))
        hp = ctx.enter_context(nc.psum_tensor("hp", [128, 512], F32))
        lp = ctx.enter_context(nc.psum_tensor("lp", [128, 512], F32))

        s_small = sem("biases_and_parameters_loaded")
        s_cload = sem("constants_loaded")
        s_wload = sem("weights_loaded")
        s_fill = sem("constant_fills_done")
        s_h16 = sem("hadamard_fp16_ready")
        s_wmean = sem("weight_means_ready")
        s_wcen = sem("weights_centred")
        s_whi = sem("weights_hi_ready")
        s_wlo = sem("weights_lo_ready")
        s_part = [sem(f"pair0_part{i}_loaded") for i in range(len(LOAD_PARTS))]
        s_chain = sem("dve_chain")
        s_load = sem("x_loaded")
        s_xs32 = sem("pair0_xs32_ready")
        s_xs_hi, s_xs_lo = sem("xs_hi_ready"), sem("xs_lo_ready")
        s_h = sem("h_out_ready")
        s_res = sem("residual_done")
        s_bn = [sem("bn_stats_x"), sem("bn_stats_x1")]
        s_gst = sem("gn_stats_ready")
        s_gred = sem("gn_reduced")
        s_gread = sem("gn_psum_read")
        s_gvar = sem("gn_var_ready")
        s_grs = sem("gn_rstd_ready")
        s_gn = [sem("gn1_ready"), sem("gn2_ready")]
        s_hbias, s_bias = sem("h_bias_ready"), sem("layer1_bias_ready")
        s_x1_hi, s_x1_lo = sem("x1_hi_ready"), sem("x1_lo_ready")
        s_mm = [sem(f"mm{n}_done") for n in (1, 2)]
        s_ssq = [sem(f"ssq{n}_ready") for n in (1, 2)]
        s_rs = [sem(f"rstd{n}_ready") for n in (1, 2)]
        s_z = [sem(f"z{n}_ready") for n in (1, 2)]
        s_tp = [sem(f"transposed{n}") for n in (1, 2)]
        s_ge = [sem(f"gelu{n}_done") for n in (1, 2)]
        s_ge_hi = [sem(f"gelu_hi{n}_ready") for n in (1, 2)]
        s_ge_lo = [sem(f"gelu_lo{n}_ready") for n in (1, 2)]
        s_l3 = sem("l3_out_ready")
        s_fin = sem("out_ready")
        s_store = sem("stored")

        s_passed = {e.engine: sem(f"waits_passed_{n}")
                    for n, e in enumerate((nc.scalar, nc.vector, nc.gpsimd))}

        def later(value):
            return not isinstance(value, int) or value > 0

        def passed(eng, value):
            if not isinstance(value, int):
                eng.sem_inc(s_passed[eng.engine], 1)

        def xcols(p, b, u):
            return X[:, bass.ds((p % NX) * SLOT + b * BLK + u * UT, UT)]

        def freed(g, u):
            return g + 1 - {0: 1, 1: 3}.get(u, 2)

        def prev(p, u, d):
            return U * p + u - d, (u - d) % U

        def exists(p, u, layer):
            if not isinstance(p, int):
                return True
            return 0 <= U * p + u + 1 - layer < U * PAIRS

        def job(p, u, n, kind):
            at = (PLAN0 if isinstance(p, int) and p == 0 else PLAN).get((u, n), {}).get(kind)
            if at is None or isinstance(p, int) and p + at[0] >= PAIRS:
                return None
            return p + at[0], at[1]

        def before_start(at):
            return not isinstance(at[0], int) or at[0] >= 0

        def h_bank(q, c, b):
            if isinstance(q, int) and q == 0:
                return (hp, lp)[(3 * c + b) % 2], 1
            return hp, 0

        def tm_bank(u, n, k):
            return (8 * u + 4 * n + k) % TM_BANKS

        def tm_before(p, u, n, k):
            pos = 8 * u + 4 * n + k
            d = {0: 2, 1: 2, 2: 5}.get(pos, 3)
            while True:
                at = pos - d
                up, off = at // 8, at % 8
                g = U * p + up
                n0, k0 = off // 4, off % 4
                if isinstance(g, int):
                    if g < 0:
                        return None
                    if not 0 <= g - n0 < U * PAIRS:
                        d += 3 if at >= 3 else {0: 2, 1: 2, 2: 5}.get(at, 3)
                        continue
                return s_z[n0], K * (g - n0) + k0 + 1

        stage = X[:, 2 * SLOT:3 * SLOT]
        wst = [stage[:, n * 768:(n + 1) * 768].rearrange("p (b o) -> p b o", b=4) for n in (0, 1)]
        w12st = stage[:, 0:1536].rearrange("p (b o) -> p b o", b=8)
        w3st = stage[:, 1536:2304].rearrange("p (b o) -> p b o", b=6)
        bst = stage[:, 2304:2304 + 4 * C].rearrange("p (n i o) -> p n i o", n=2, i=2)
        bscr = stage[:, 2304 + 4 * C:2304 + 8 * C].rearrange("p (n i o) -> p n i o", n=2, i=2)
        xs32 = stage[:, 4096:4096 + 6 * UT].rearrange("p (a b t) -> p a b t", a=2, b=3)
        escr = stage[0:2, 2304 + 8 * C:2308 + 8 * C].rearrange("p (n i) -> p n i", n=2)

        block = ctx.enter_context(nc.Block())

        @block.sync
        def _(sp):
            def load(p):
                sp.dma_start(X[:, bass.ds((p % NX) * SLOT, 2 * BLK)].rearrange("c (i t) -> c i t", i=2),
                             x[bass.ds(2 * p, 2), 0:CA, :].rearrange("i c t -> c i t")).then_inc(s_load, 16)
                for i in range(2):
                    sp.dma_start(X[i * CC:(i + 1) * CC, bass.ds((p % NX) * SLOT + 2 * BLK, BLK)],
                                 x[bass.ds(2 * p + i, 1), CA:C, :].rearrange("i c t -> c (i t)")).then_inc(s_load, 16)

            def store(p, u):
                sp.wait_ge(s_fin, 3 * (U * p + u + 1))
                t0 = u * UT
                sp.dma_start(out[bass.ds(2 * p, 2), 0:CA, t0:t0 + UT].rearrange("i c t -> c i t"),
                             X[:, bass.ds((p % NX) * SLOT, 2 * BLK)].rearrange("c (i t) -> c i t", i=2)[:, :, t0:t0 + UT]
                             ).then_inc(s_store, 16)
                for i in range(2):
                    sp.dma_start(out[bass.ds(2 * p + i, 1), CA:C, t0:t0 + UT].rearrange("i c t -> c (i t)"),
                                 X[i * CC:(i + 1) * CC, bass.ds((p % NX) * SLOT + 2 * BLK + t0, UT)]
                                 ).then_inc(s_store, 16)

            sp.dma_start(par[:, :], params).then_inc(s_small, 16)
            sp.dma_start(bst[0:2].rearrange("p n i o -> p (n i o)"), biases).then_inc(s_small, 16)
            for part, units in enumerate(LOAD_PARTS):
                t0, n = units[0] * UT, len(units) * UT
                sp.dma_start(X[:, 0:2 * BLK].rearrange("c (i t) -> c i t", i=2)[:, :, t0:t0 + n],
                             x[0:2, 0:CA, t0:t0 + n].rearrange("i c t -> c i t")).then_inc(s_part[part], 16)
                for i in range(2):
                    sp.dma_start(X[i * CC:(i + 1) * CC, 2 * BLK + t0:2 * BLK + t0 + n],
                                 x[i:i + 1, CA:C, t0:t0 + n].rearrange("i c t -> c (i t)")).then_inc(s_part[part], 16)
            sp.dma_start(cst[:, :], consts).then_inc(s_cload, 16)
            sp.dma_start(stage[:, 0:2304], weights).then_inc(s_wload, 16)
            load(1)
            sp.wait_ge(s_wlo, 3)
            sp.wait_ge(s_load, 48)
            load(2)

            def stores(p):
                for u in range(U):
                    store(p, u)

            with sp.Fori(0, PAIRS - NX) as p:
                stores(p)
                sp.wait_ge(s_store, 48 * U * (p + 1))
                load(p + NX)
            with sp.Fori(PAIRS - NX, PAIRS) as p:
                stores(p)
            sp.wait_ge(s_store, 48 * U * PAIRS)

        @block.tensor
        def _(pe):
            def gn_reduce(j):
                pe.wait_ge(s_gst, j + 1)
                for b, terms in enumerate((((AA, 0), (CIA, 2)), ((AA, 1), (CJA, 2)), ((AIC, 0), (AJC, 1), (CCB, 2)))):
                    for i, (m, src) in enumerate(terms):
                        last = nc.tensor.matmul(hp[:, 2 * b:2 * b + 2], group_mean[:, m, :], gst[:, :, src],
                                                start=(i == 0), stop=(i == len(terms) - 1))
                last.then_inc(s_gred, 1)

            def gn1(q):
                if later(GREADS * q):
                    pe.wait_ge(s_gread, GREADS * q)
                gn_reduce(2 * q)

            def h_shift(q):
                pe.wait_ge(s_gread, GREADS * q + 1)
                pe.wait_ge(s_gn[0], q + 1)
                for b, terms in enumerate((((AA, 0), (CIA, 2)), ((AA, 1), (CJA, 2)), ((AIC, 0), (AJC, 1), (CCB, 2)))):
                    for i, (m, src) in enumerate(terms):
                        last = nc.tensor.matmul(hp[:, b:b + 1], h32[:, m, :], gshift[0][:, src, 0:1],
                                                start=(i == 0), stop=(i == len(terms) - 1))
                last.then_inc(s_gred, 1)

            def gn2(q):
                pe.wait_ge(s_res, 21 * (q + 1))
                gn_reduce(2 * q + 1)

            def w1_shift(q):
                pe.wait_ge(s_gread, GREADS * q + 3)
                pe.wait_ge(s_gn[1], q + 1)
                for i, terms in enumerate((((0, 0), (1, 2)), ((3, 1), (2, 2)))):
                    for r, (rows, src) in enumerate(terms):
                        last = nc.tensor.matmul(hp[0:2, i * C:(i + 1) * C], gshift[1][:, src, :], w32[:, rows, :],
                                                start=(r == 0), stop=(r == 1))
                last.then_inc(s_gred, 1)

            def h_out(q, c, b):
                a = U * q + c
                bank, ahead = h_bank(q, c, b)
                if b == 0:
                    pe.wait_ge(s_xs_lo, a + 1)
                if c == 0 and b == 0:
                    pe.wait_ge(s_gread, GREADS * q + 2)
                else:
                    if later(3 * a + b - ahead):
                        pe.wait_ge(s_res, 3 * a + b - ahead)
                hi, lo = xs_hi[:, c % 2], xs_lo[:, c % 2]
                if b < 2:
                    terms = [(AA, b, 0, 128), ((CIA, CJA)[b], 2, 0, 128)]
                else:
                    terms = [(CCB, 2, 0, 128), (AIC, 0, 0, 64), (AJC, 1, 64, 128)]
                n = 0
                for m, src, lo_p, hi_p in terms:
                    for part in (hi, lo):
                        last = nc.tensor.matmul(bank[lo_p:hi_p, 0:UT], h16[:, m, lo_p:hi_p], part[:, src, :],
                                                start=(n == 0), stop=(m in ((CIA, CJA) if b < 2 else (AIC, AJC)) and part is lo),
                                                skip_group_check=True)
                        n += 1
                last.then_inc(s_h, 1)

            def group(p, u, n, k):
                g, un = prev(p, u, n)
                if k == 0:
                    pe.wait_ge((s_x1_lo, s_ge_lo[0])[n], g + 1)
                    if n == 0 and u == 0:
                        pe.wait_ge(s_bias, p + 1)
                before = tm_before(p, u, n, k)
                if before:
                    pe.wait_ge(*before)
                dst = tm[tm_bank(u, n, k)]
                hi, lo = ((x1_hi, x1_lo), (ge_hi[0], ge_lo[0]))[n]
                cols = slice(k * TT, (k + 1) * TT)
                nc.tensor.matmul(dst[:, :, :], ones[:, :], bias_rows[n][:, :, :], start=True, stop=False,
                                 skip_group_check=True)
                for act, w in ((hi, w_hi[n]), (hi, w_lo[n]), (lo, w_hi[n])):
                    nc.tensor.matmul(dst[:, :, 0:C], act[:, un % 2, 2, cols], w[:, 1:3, :], start=False, stop=False,
                                     skip_group_check=True)
                for i in range(2):
                    for r, (act, w) in enumerate(((hi, w_hi[n]), (hi, w_lo[n]), (lo, w_hi[n]))):
                        last = nc.tensor.matmul(dst[:, i, 0:C], act[:, un % 2, i, cols], w[:, 3 * i, :], start=False,
                                                stop=(r == 2), skip_group_check=True)
                last.then_inc(s_mm[n], 1)

            def transposes(p, u, n, k):
                g, _ = prev(p, u, n)
                if k == 0:
                    if n == 0:
                        if later(2 * (g - 1)):
                            pe.wait_ge(s_ge[1], 2 * (g - 1))
                    else:
                        pe.wait_ge(s_ge[0], 2 * min(g + 2, U * PAIRS) if isinstance(g, int) else 2 * (g + 2))
                pe.wait_ge(s_z[n], K * g + k + 1)
                cols = slice(k * TT, (k + 1) * TT)
                for blk, at in ((0, 0), (1, C + CC), (2, CA)):
                    last = nc.tensor.transpose(tp[:, blk, cols], z[n][:, k, at:at + 128], ident[0:TT, 0:TT])
                if k == K - 1:
                    last.then_inc(s_tp[n], 1)

            def l3_out(p, u, b):
                g, u3 = prev(p, u, 2)
                if b == 0:
                    pe.wait_ge(s_ge_lo[1], g + 1)
                if later(3 * g + b):
                    pe.wait_ge(s_fin, 3 * g + b)
                hi, lo = ge_hi[1][:, u3 % 2], ge_lo[1][:, u3 % 2]
                if b < 2:
                    terms = [(AA, b, 0, 128), ((CIA, CJA)[b], 2, 0, 128)]
                else:
                    terms = [(CCB, 2, 0, 128), (AIC, 0, 0, 64), (AJC, 1, 64, 128)]
                ends = (CIA, CJA) if b < 2 else (AIC, AJC)
                n = 0
                for m, src, lo_p, hi_p in terms:
                    for r, (w, act) in enumerate(((w3_hi, hi), (w3_hi, lo), (w3_lo, hi))):
                        last = nc.tensor.matmul(lp[lo_p:hi_p, 0:UT], w[:, m, lo_p:hi_p], act[:, src, :],
                                                start=(n == 0), stop=(m in ends and r == 2), skip_group_check=True)
                        n += 1
                last.then_inc(s_l3, 1)

            def half(p, u, n):
                have = exists(p, u, n + 1)
                h, gn = job(p, u, n, "h"), job(p, u, n, "gn")
                late = ((p, u - 1, 1) if u > 0 else (p - 1, U - 1, 1)) if n == 0 else (p, u, 0)

                def between(i):
                    if h:
                        h_out(*h, i)
                    if n == 1 and exists(p, u, 3):
                        l3_out(p, u, i)
                    if gn and i == 0:
                        (gn1, gn2)[gn[1]](gn[0])
                    if gn and i == 2:
                        (h_shift, w1_shift)[gn[1]](gn[0])

                if have:
                    group(p, u, n, 0)
                if before_start(late) and exists(late[0], late[1], late[2] + 1):
                    transposes(*late, 3)
                if have:
                    group(p, u, n, 1)
                between(0)
                if have:
                    group(p, u, n, 2)
                    transposes(p, u, n, 0)
                between(1)
                if have:
                    group(p, u, n, 3)
                    transposes(p, u, n, 1)
                between(2)
                if have:
                    transposes(p, u, n, 2)

            def step(p, u):
                half(p, u, 0)
                half(p, u, 1)

            pe.wait_ge(s_cload, 16)
            gn1(0)
            h_shift(0)
            pe.wait_ge(s_h16, 1)
            for c in range(U):
                for b in range(3):
                    h_out(0, c, b)
            gn2(0)
            pe.wait_ge(s_wcen, 1)
            w1_shift(0)
            pe.wait_ge(s_fill, 1)
            pe.wait_ge(s_wlo, 3)
            run(pe, step)

        @block.scalar
        def _(act):
            def scaled_hi(q, c):
                a = U * q + c
                if c == 0:
                    act.wait_ge(s_gn[0], q + 1)
                if later(3 * freed(a, c)):
                    act.wait_ge(s_h, 3 * freed(a, c))
                    passed(act, 3 * freed(a, c))
                for b in range(3):
                    last = nc.scalar.activation(xs_hi[:, c % 2, b, :], xcols(q, b, c), ACT.Copy,
                                                scale=gscale[0][:, b:b + 1])
                last.then_inc(s_xs_hi, 1)

            def split_x1(p, u):
                g = U * p + u
                if u == 0:
                    act.wait_ge(s_gn[1], p + 1)
                if later(K * freed(g, u)):
                    act.wait_ge(s_mm[0], K * freed(g, u))
                    passed(act, K * freed(g, u))
                for b in range(3):
                    last = nc.scalar.activation(x1_hi[:, u % 2, b, :], xcols(p, b, u), ACT.Copy,
                                                scale=gscale[1][:, b:b + 1])
                last.then_inc(s_x1_hi, 1)

            def squares(p, u, n, k):
                g, _ = prev(p, u, n)
                act.wait_ge(s_mm[n], K * g + k + 1)
                for i in range(2):
                    last = nc.scalar.activation(z[n][:, k, i * TW:(i + 1) * TW], tm[tm_bank(u, n, k)][:, i, :], ACT.Square,
                                                scale=float(C) ** -0.5,
                                                accum_out=ssq[n][:, k, i:i + 1])
                last.then_inc(s_ssq[n], 1)

            def gelu(p, u, n):
                g, _ = prev(p, u, n)
                act.wait_ge(s_tp[n], g + 1)
                if later(g):
                    act.wait_ge(s_ge_lo[n], g)
                for blocks, c in ((slice(0, 2), 0), (slice(2, 3), 1)):
                    nc.scalar.activation(ge[n][:, blocks, :], tp[:, blocks, 0:UT], ACT.Gelu,
                                         bias=par[:, 4 * n + 2 + c:4 * n + 3 + c],
                                         scale=par[:, 4 * n + c:4 * n + c + 1]).then_inc(s_ge[n], 1)

            def gelu_hi(g, un, n):
                act.wait_ge(s_ge[n], 2 * (g + 1))
                if later((K, 3)[n] * freed(g, un)):
                    act.wait_ge((s_mm[1], s_l3)[n], (K, 3)[n] * freed(g, un))
                nc.scalar.activation(ge_hi[n][:, un % 2], ge[n][:, :, :], ACT.Copy).then_inc(s_ge_hi[n], 1)

            def half(p, u, n):
                have = exists(p, u, n + 1)
                late = ((p, u - 1, 1) if u > 0 else (p - 1, U - 1, 1)) if n == 0 else (p, u, 0)
                have_late = before_start(late) and exists(late[0], late[1], late[2] + 1)
                if n == 1:
                    if u < U - 1 and exists(p, u, 1):
                        split_x1(p, u + 1)
                    elif not isinstance(p, int) or p + 1 < PAIRS:
                        split_x1(p + 1, 0)
                for k in range(K):
                    if have:
                        squares(p, u, n, k)
                    if k == 0 and have_late:
                        gelu(*late)
                    if k == 2 and have_late:
                        gelu_hi(*prev(*late), late[2])
                hi = job(p, u, n, "hi")
                if hi:
                    scaled_hi(*hi)

            def step(p, u):
                half(p, u, 0)
                half(p, u, 1)

            def centre(n):
                act.wait_ge(s_wmean, 2)
                for b in range(4):
                    last = nc.scalar.activation((w32, wst[1])[n][:, b, :], wst[n][:, b, :], ACT.Identity,
                                                bias=wsum[:, 4 * n + b:4 * n + b + 1], scale=W_SCALE)
                last.then_inc(s_wcen, 1)

            def weights_hi(n):
                act.wait_ge(s_wcen, n + 1)
                nc.scalar.activation((w_hi[0], w_hi[1], w3_hi)[n][:, :, :], (w32[:, :, :], wst[1], w3st)[n],
                                     ACT.Copy).then_inc(s_whi, 1)

            def first_hi(c):
                if c == 0:
                    act.wait_ge(s_gn[0], 1)
                if c >= 2:
                    act.wait_ge(s_xs_lo, c - 1)
                for b in range(3):
                    last = nc.scalar.activation(xs32[:, c % 2, b, :], xcols(0, b, c), ACT.Copy,
                                                scale=gscale[0][:, b:b + 1])
                last.then_inc(s_xs32, 1)
                if c >= 2:
                    act.wait_ge(s_h, 3 * (c - 1))
                act.wait_ge(s_xs32, c + 1)
                nc.scalar.activation(xs_hi[:, c % 2], xs32[:, c % 2], ACT.Copy).then_inc(s_xs_hi, 1)

            act.wait_ge(s_small, 32)
            act.wait_ge(s_cload, 16)
            nc.scalar.activation(h16[:, :, :], h32, ACT.Copy).then_inc(s_h16, 1)
            for c in range(U):
                first_hi(c)
                if c == 2:
                    centre(0)
                    weights_hi(0)
                if c == 3:
                    centre(1)
                    weights_hi(1)
                if c == 4:
                    nc.scalar.activation(w3st, w3st, ACT.Copy, scale=W_SCALE).then_inc(s_wcen, 1)
                    weights_hi(2)
            split_x1(0, 0)
            run(act, step)

        @block.gpsimd
        def _(pool):
            def gn(q, n):
                pool.wait_ge(s_gvar, 2 * q + n + 1)
                nc.gpsimd.tensor_tensor(gscale[n][:, :], gvar[:, :], neg_half[:, 0:3], ALU.pow).then_inc(s_grs, 1)

            def rstd(p, u, n, k):
                g, _ = prev(p, u, n)
                pool.wait_ge(s_ssq[n], K * g + k + 1)
                nc.gpsimd.tensor_tensor(rs[n][:, k, :], ssq[n][:, k, :], neg_half[0:TT, 0:2],
                                        ALU.pow).then_inc(s_rs[n], 1)

            def gelu_lo(g, un, n):
                pool.wait_ge(s_ge_hi[n], g + 1)
                for b in range(3):
                    last = nc.gpsimd.tensor_tensor(ge_lo[n][:, un % 2, b, :], ge[n][:, b, :],
                                                   ge_hi[n][:, un % 2, b, :], ALU.subtract)
                last.then_inc(s_ge_lo[n], 1)

            def half(p, u, n):
                norm = job(p, u, n, "gn")
                late = ((p, u - 1, 1) if u > 0 else (p - 1, U - 1, 1)) if n == 0 else (p, u, 0)
                for k in range(K):
                    if exists(p, u, n + 1):
                        rstd(p, u, n, k)
                    if norm and k == 1:
                        gn(*norm)
                if before_start(late) and exists(late[0], late[1], late[2] + 1):
                    gelu_lo(*prev(*late), late[2])

            def step(p, u):
                half(p, u, 0)
                half(p, u, 1)

            def first_lo(c):
                pool.wait_ge(s_xs_hi, c + 1)
                for b in range(3):
                    last = nc.gpsimd.tensor_tensor(xs_lo[:, c % 2, b, :], xs32[:, c % 2, b, :],
                                                   xs_hi[:, c % 2, b, :], ALU.subtract)
                last.then_inc(s_xs_lo, 1)

            pool.wait_ge(s_fill, 1)
            gn(0, 0)
            for c in range(U):
                first_lo(c)
            for n in range(2):
                pool.wait_ge(s_whi, n + 1)
                nc.gpsimd.tensor_tensor(w_lo[n][:, :, :], (w32[:, :, :], wst[1])[n], w_hi[n][:, :, :],
                                        ALU.subtract).then_inc(s_wlo, 1)
            gn(0, 1)
            pool.wait_ge(s_whi, 3)
            nc.gpsimd.tensor_tensor(w3_lo[:, :, :], w3st, w3_hi[:, :, :], ALU.subtract).then_inc(s_wlo, 1)
            run(pool, step)

        @block.vector
        def _(dve):
            links = {"at": 0}

            def link(ins):
                links["at"] += 1
                ins.then_inc(s_chain, 1)
                dve.wait_ge(s_chain, links["at"])

            def fills():
                for n in range(2):
                    nc.vector.memset(bias_rows[n][:, :, :], 0.0)
                nc.vector.memset(ones[:, :], 1.0)
                nc.vector.memset(neg_half[:, :], -0.5).then_inc(s_fill, 1)
                dve.wait_ge(s_fill, 1)

            def split_bias(n, value, scratch):
                dst = bias_rows[n][0:2, :, 0:C]
                link(nc.vector.tensor_copy(dst, value))
                link(nc.vector.scalar_tensor_tensor(out=scratch, in0=dst, scalar=row1[0:2, :], in1=value,
                                                    op0=ALU.mult, op1=ALU.subtract))
                link(nc.vector.tensor_scalar(dst, scratch, -1.0, None, ALU.mult))

            def layer_biases():
                dve.wait_ge(s_small, 32)
                link(nc.vector.reduce_sum(bsum[:, :], bst[0:2, :, 0, :], axis=AX.X))
                link(nc.vector.tensor_scalar(bsum[:, :], bsum[:, :], -1.0 / C, None, ALU.mult))
                nc.vector.tensor_scalar(b32[:, :, :], bst[0:2, 0], bsum[:, 0:1], W_SCALE, ALU.add, ALU.mult)
                link(nc.vector.tensor_scalar(bscr[0:2, 0], bst[0:2, 1], bsum[:, 1:2], W_SCALE, ALU.add, ALU.mult))
                split_bias(1, bscr[0:2, 0], bscr[0:2, 1])
                link(nc.vector.memset(escr[:, 0], (C * LN_EPS) ** 0.5 * W_SCALE))
                link(nc.vector.tensor_copy(bias_rows[0][0:2, :, C], escr[:, 0]))
                link(nc.vector.scalar_tensor_tensor(out=escr[:, 1], in0=bias_rows[0][0:2, :, C], scalar=row1[0:2, :],
                                                    in1=escr[:, 0], op0=ALU.mult, op1=ALU.subtract))
                for n in range(2):
                    last = nc.vector.tensor_scalar(bias_rows[n][0:2, :, C], escr[:, 1], -1.0, None, ALU.mult)
                link(last)

            def weight_means():
                dve.wait_ge(s_wload, 16)
                nc.vector.reduce_sum(wsum[:, :], w12st, axis=AX.X).then_inc(s_wmean, 1)
                dve.wait_ge(s_wmean, 1)
                nc.vector.tensor_scalar(wsum[:, :], wsum[:, :], -W_SCALE / C, None, ALU.mult).then_inc(s_wmean, 1)

            def first_stats():
                for part, units in enumerate(LOAD_PARTS):
                    dve.wait_ge(s_part[part], 48)
                    for c in units:
                        for b in range(3):
                            last = nc.vector.bn_stats(bn[0][:, b, c, :], xcols(0, b, c))
                        last.then_inc(s_bn[0], 1)

            def stats_x(q, cs):
                if cs[0] == 0:
                    dve.wait_ge(s_load, 48 * q)
                    passed(dve, 48 * q)
                for c in cs:
                    for b in range(3):
                        last = nc.vector.bn_stats(bn[0][:, b, c, :], xcols(q, b, c))
                    last.then_inc(s_bn[0], 1)

            def scaled_lo(q, c):
                a = U * q + c
                dve.wait_ge(s_xs_hi, a + 1)
                for b in range(3):
                    last = nc.vector.scalar_tensor_tensor(out=xs_lo[:, c % 2, b, :], in0=xcols(q, b, c),
                                                          scalar=gscale[0][:, b:b + 1], in1=xs_hi[:, c % 2, b, :],
                                                          op0=ALU.mult, op1=ALU.subtract)
                last.then_inc(s_xs_lo, 1)

            def residual(q, c, b):
                r = 3 * (U * q + c) + b + 1
                dve.wait_ge(s_h, r)
                nc.vector.scalar_tensor_tensor(out=xcols(q, b, c), in0=h_bank(q, c, b)[0][:, 0:UT], scalar=h_bias[:, b:b + 1],
                                               in1=xcols(q, b, c), op0=ALU.add, op1=ALU.add).then_inc(s_res, 1)

            def stats_x1(q, c):
                dve.wait_ge(s_res, 3 * (U * q + c) + 3)
                passed(dve, 3 * (U * q + c) + 3)
                for b in range(3):
                    last = nc.vector.bn_stats(bn[1][:, b, c, :], xcols(q, b, c))
                last.then_inc(s_bn[1], 1)

            LINKS = ((2, 2, 0, 0), (3, 2, 1, 2))
            PER_PAIR = sum(map(sum, LINKS))

            def chain(q, n, stage):
                first = BASE + PER_PAIR * q + n * sum(LINKS[0]) + sum(LINKS[n][:stage])
                at = [0]

                def do(ins):
                    at[0] += 1
                    ins.then_inc(s_chain, 1)
                    dve.wait_ge(s_chain, first + at[0])

                return do

            def gn_stats(q, n):
                do = chain(q, n, 0)
                dve.wait_ge(s_bn[n], U * (q + 1))
                passed(dve, U * (q + 1))
                for b in range(3):
                    last = nc.vector.bn_aggr(gst[:, :, b], bn[n][:, b, :, :].rearrange("p u s -> p (u s)"))
                do(last)
                if n == 1:
                    do(nc.vector.tensor_tensor(gst[:, 0, :], gst[:, 0, :], par[:, 8:11], ALU.subtract))
                do(nc.vector.tensor_tensor(gsq[:, :], gst[:, 0, :], gst[:, 0, :], ALU.mult))
                nc.vector.tensor_tensor(gst[:, 1, :], gst[:, 1, :], gsq[:, :], ALU.add).then_inc(s_gst, 1)

            def gn_var(q, n):
                do = chain(q, n, 1)
                reads = GREADS * q + 2 * n + 1
                dve.wait_ge(s_gred, reads)
                nc.vector.tensor_copy(gmu[:, :, :], hp[:, 0:6].rearrange("p (b s) -> p b s", b=3)).then_inc(s_gread, 1)
                dve.wait_ge(s_gread, reads)
                do(nc.vector.tensor_tensor(gsq[:, :], gmu[:, :, 0], gmu[:, :, 0], ALU.mult))
                do(nc.vector.tensor_tensor(gvar[:, :], gmu[:, :, 1], gsq[:, :], ALU.subtract))
                nc.vector.tensor_scalar(gvar[:, :], gvar[:, :], 0.0, GN_EPS, ALU.max, ALU.add).then_inc(s_gvar, 1)

            def gn_shift(q, n):
                do = chain(q, n, 2)
                dve.wait_ge(s_grs, 2 * q + n + 1)
                mu = gmu[:, :, 0]
                if n == 1:
                    do(nc.vector.tensor_tensor(gsq[:, :], mu, par[:, 8:11], ALU.add))
                    mu = gsq[:, :]
                for i in range(2):
                    last = nc.vector.scalar_tensor_tensor(out=gshift[n][:, :, i], in0=mu, scalar=-1.0,
                                                          in1=gscale[n][:, :], op0=ALU.mult, op1=ALU.mult)
                last.then_inc(s_gn[n], 1)

            def gn_bias(q, n):
                reads = GREADS * q + 2 * n + 2
                dve.wait_ge(s_gred, reads)
                if n == 0:
                    nc.vector.tensor_tensor(h_bias[:, :], hp[:, 0:3], par[:, 8:11], ALU.add).then_inc(s_gread, 1)
                    dve.wait_ge(s_gread, reads)
                    return
                do = chain(q, n, 3)
                nc.vector.tensor_tensor(b_row[:, :, :], hp[0:2, 0:2 * C].rearrange("p (i o) -> p i o", i=2),
                                        b32[:, :, :], ALU.add).then_inc(s_gread, 1)
                dve.wait_ge(s_gread, reads)
                dst = bias_rows[0][0:2, :, 0:C]
                do(nc.vector.tensor_copy(dst, b_row[:, :, :]))
                do(nc.vector.scalar_tensor_tensor(out=b_row[:, :, :], in0=dst, scalar=row1[0:2, :], in1=b_row[:, :, :],
                                                  op0=ALU.mult, op1=ALU.subtract))
                nc.vector.tensor_scalar(dst, b_row[:, :, :], -1.0, None, ALU.mult).then_inc(s_bias, 1)

            def x1_split_lo(p, u):
                g = U * p + u
                dve.wait_ge(s_x1_hi, g + 1)
                for b in range(3):
                    last = nc.vector.scalar_tensor_tensor(out=x1_lo[:, u % 2, b, :], in0=xcols(p, b, u),
                                                          scalar=gscale[1][:, b:b + 1], in1=x1_hi[:, u % 2, b, :],
                                                          op0=ALU.mult, op1=ALU.subtract)
                last.then_inc(s_x1_lo, 1)

            def normalise(p, u, n, k):
                g, _ = prev(p, u, n)
                dve.wait_ge(s_rs[n], K * g + k + 1)
                nc.vector.tensor_tensor(z[n][:, k, 0:2 * C].rearrange("p (i o) -> p i o", i=2),
                                        tm[tm_bank(u, n, k)][:, :, 0:C],
                                        rs[n][:, k, :].unsqueeze(2).to_broadcast([TT, 2, C]),
                                        ALU.mult).then_inc(s_z[n], 1)

            def final(p, u, b):
                g, u3 = prev(p, u, 2)
                pp = p if u >= 2 else p - 1
                dve.wait_ge(s_l3, 3 * g + b + 1)
                nc.vector.scalar_tensor_tensor(out=xcols(pp, b, u3), in0=lp[:, 0:UT], scalar=1.0 / W_SCALE,
                                               in1=xcols(pp, b, u3), op0=ALU.mult, op1=ALU.add).then_inc(s_fin, 1)

            def half(p, u, n):
                have, have3 = exists(p, u, n + 1), n == 1 and exists(p, u, 3)
                h, gn, stats = (job(p, u, n, kind) for kind in ("h", "gn", "stats_x"))
                before, after = job(p, u, n, "stats_x1_before"), job(p, u, n, "stats_x1")
                lo, gathered = job(p, u, n, "lo"), job(p, u, n, "gn_stats")
                if before:
                    stats_x1(*before)
                for k in range(K):
                    if have:
                        normalise(p, u, n, k)
                    if k != 1:
                        b = (0, None, 1, 2)[k]
                        if h:
                            residual(*h, b)
                        if have3:
                            final(p, u, b)
                    if gn and k != 2:
                        (gn_var, gn_shift, None, gn_bias)[k](*gn)
                    if k == 0 and stats:
                        stats_x(stats[0], stats[1][:1])
                    if k == 0 and n == 1:
                        if u < U - 1 and exists(p, u, 1):
                            x1_split_lo(p, u + 1)
                        elif not isinstance(p, int) or p + 1 < PAIRS:
                            x1_split_lo(p + 1, 0)
                    if k == 2 and stats and stats[1][1:]:
                        stats_x(stats[0], stats[1][1:])
                if lo:
                    scaled_lo(*lo)
                if after:
                    stats_x1(*after)
                if gathered:
                    gn_stats(*gathered)

            def step(p, u):
                half(p, u, 0)
                half(p, u, 1)

            fills()
            layer_biases()
            BASE = links["at"]
            first_stats()
            for part in (gn_stats, gn_var, gn_shift, gn_bias):
                part(0, 0)
            for c in range(U):
                for b in range(3):
                    residual(0, c, b)
                    if b == 0 and c > 0:
                        stats_x1(0, c - 1)
                if c == 0:
                    weight_means()
            stats_x1(0, U - 1)
            for part in (gn_stats, gn_var, gn_shift, gn_bias):
                part(0, 1)
            x1_split_lo(0, 0)
            run(dve, step)


def run(eng, step):
    for u in range(U):
        step(0, u)
    with eng.Fori(1, PAIRS - 2) as p:
        for u in range(U):
            step(p, u)
    for p in (PAIRS - 2, PAIRS - 1):
        for u in range(U):
            step(p, u)
    for u in range(2):
        step(PAIRS, u)


def blocks6(m):
    r = np.zeros((128, 6, 128), np.float32)
    r[:, AA] = m[:CA, :CA]
    r[:CC, CIA] = m[CA:, :CA]
    r[CC:, CJA] = m[CA:, :CA]
    r[:, AIC, :CC] = m[:CA, CA:]
    r[:, AJC, CC:] = m[:CA, CA:]
    r[:CC, CCB, :CC] = m[CA:, CA:]
    r[CC:, CCB, CC:] = m[CA:, CA:]
    return r.reshape(128, 768)


def blocks4(m):
    j = np.concatenate([m[:, CA:], m[:, :CA]], axis=1)
    r = np.zeros((128, 4, C), np.float32)
    r[:, 0] = m[:CA]
    r[:CC, 1] = m[CA:]
    r[CC:, 2] = j[CA:]
    r[:, 3] = j[:CA]
    return r.reshape(128, 4 * C)


def bias_layout(b1, b2):
    r = np.concatenate([p for b in (b1, b2) for p in (b, b[CA:], b[:CA])])
    return np.ascontiguousarray(np.broadcast_to(r, (2, 4 * C)))


def param_layout(g1, be1, g2, be2, b3):
    cols = [c for v in (g1, be1, g2, be2) for c in (v[:CA], np.tile(v[CA:], 2))]
    cols += [b3[:CA], b3[:CA], np.tile(b3[CA:], 2), (np.arange(128) == 1).astype(np.float32)]
    return np.ascontiguousarray(np.stack(cols, axis=1))


def constants():
    had = np.array([[1.0]], np.float32)
    while had.shape[0] < 256:
        had = np.block([[had, had], [had, -had]])
    had = (had / 16.0)[:C, :C].astype(np.float32)
    ch = np.arange(C)
    grp = (ch[:, None] // GROUP == ch[None, :] // GROUP).astype(np.float32) / np.float32(GROUP)
    return np.concatenate([blocks6(grp), blocks6(had), np.eye(128, dtype=np.float32)], axis=1)


def kernel(x, L1_conv_W1, L1_conv_b1, L1_conv_g1, L1_conv_beta1, L1_conv_W2, L1_conv_b2,
           L1_conv_g2, L1_conv_beta2, L1_conv_W3, L1_conv_b3):
    import concourse.bacc as bacc
    from concourse.bass_utils import run_bass_kernel_spmd

    x = np.asarray(x)
    w1t, w2t, w3t = (np.asarray(w).T for w in (L1_conv_W1, L1_conv_W2, L1_conv_W3))
    arrays = {
        "x": np.ascontiguousarray(x.reshape(B, C, HW)),
        "weights": np.concatenate([blocks4(w1t), blocks4(w2t), blocks6(w3t)], axis=1),
        "biases": bias_layout(np.asarray(L1_conv_b1), np.asarray(L1_conv_b2)),
        "params": param_layout(np.asarray(L1_conv_g1), np.asarray(L1_conv_beta1), np.asarray(L1_conv_g2),
                               np.asarray(L1_conv_beta2), np.asarray(L1_conv_b3)),
        "consts": constants(),
    }
    nc = bacc.Bacc("TRN2", target_bir_lowering=False, num_devices=1)
    args = [nc.dram_tensor(n, a.shape, mybir.dt.from_np(a.dtype), kind="ExternalInput").ap()
            for n, a in arrays.items()]
    out = nc.dram_tensor("out", (B, C, HW), F32, kind="ExternalOutput").ap()
    build(nc, *args, out)
    r = run_bass_kernel_spmd(nc, [arrays], core_ids=[0])
    return r.results[0]["out"].reshape(x.shape)
```

```python
from contextlib import ExitStack

import numpy as np
import concourse.bass as bass
from concourse import mybir

F32, F16 = mybir.dt.float32, mybir.dt.float16
ACT = mybir.ActivationFunctionType
ALU = mybir.AluOpType
AX = mybir.AxisListType

B, C, HW = 16, 192, 56 * 56
CA, CC = 128, 64
PAIRS = B // 2
U = 7
UT = HW // U
K = 4
TT = UT // K
GROUP = C // 32
BLK = HW
SLOT = 3 * BLK
NX = 3
W_SCALE = 64.0
GN_EPS, LN_EPS = 1e-5, 1e-6
BND, BNA = 6, 2
TM_BANKS = 3
AA, CIA, CJA, AIC, AJC, CCB = range(6)
TW = C + 2
GREADS = 4
PLAN = {u: {"h": (1, u), "hi": (1, u + 1), "stats": (2, (3 * u, 3 * u + 3))} for u in range(6)}
PLAN[0]["gn_end"] = (1, 0)
PLAN[5]["h_2nd"] = (1, 6)
PLAN[6] = {"gn": (1, 1), "gn_2nd": (2, 0), "hi_end": (2, 0), "stats_early": (2, (18, 21))}
PLAN0 = {
    0: {"gn": (1, 0), "hi_end": (1, 0)},
    1: {"h": (1, 0), "hi": (1, 1)},
    2: {"h": (1, 1), "hi": (1, 2), "stats": (2, (0, 4))},
    3: {"h": (1, 2), "hi": (1, 3), "hi_end": (1, 4), "h_2nd": (1, 3), "stats": (2, (4, 8))},
    4: {"h": (1, 4), "hi_end": (1, 5), "stats": (2, (8, 12))},
    5: {"h": (1, 5), "h_2nd": (1, 6), "hi": (1, 6), "stats": (2, (12, 16))},
    6: {**PLAN[6], "stats_early": (2, (16, 21))},
}


def tm_rotation():
    banks, order = [], list(range(TM_BANKS))
    for pos in range(2 * K * U):
        order.append(order.pop(1 if pos in (8 * 2 + 7, 8 * 4 + 7) else 0))
        banks.append(order[-1])
    assert order == list(range(TM_BANKS))
    gaps = [next(d for d in range(1, len(banks)) if banks[pos - d] == bank) for pos, bank in enumerate(banks)]
    return banks, gaps


TM_BANK, TM_GAP = tm_rotation()


def build(nc, x, weights, biases, params, consts, out):
    ctx = ExitStack()
    with ctx:
        def sb(name, shape, dt):
            return ctx.enter_context(nc.sbuf_tensor(name, shape, dt))

        def sem(name):
            return ctx.enter_context(nc.semaphore(name))

        X = sb("X", [128, NX * SLOT], F32)
        xs_hi = sb("xs_hi", [128, 2, 3, UT], F16)
        xs_lo = sb("xs_lo", [128, 2, 3, UT], F16)
        x1_hi = sb("x1_hi", [128, 2, 3, UT], F16)
        x1_lo = sb("x1_lo", [128, 2, 3, UT], F16)
        z = [sb(f"z{n}", [TT, K, 2 * TW], F32) for n in (1, 2)]
        ge = [sb(f"ge{n}", [128, 3, UT], F32) for n in (1, 2)]
        ge_hi = [sb(f"ge_hi{n}", [128, 4 - n, 3, UT], F16) for n in (1, 2)]
        ge_lo = [sb(f"ge_lo{n}", [128, 4 - n, 3, UT], F16) for n in (1, 2)]
        w_hi = [sb(f"w_hi{n}", [128, 4, C], F16) for n in (1, 2)]
        w_lo = [sb(f"w_lo{n}", [128, 4, C], F16) for n in (1, 2)]
        w32 = sb("w32", [128, 4, C], F32)
        b32 = sb("b32", [2, 2, C], F32)
        b_row = sb("b_row", [2, 2, C], F32)
        w3_hi = sb("w3_hi", [128, 6, 128], F16)
        w3_lo = sb("w3_lo", [128, 6, 128], F16)
        h16 = sb("h16", [128, 6, 128], F16)
        cst = sb("cst", [128, 13 * 128], F32)
        group_mean = cst[:, 0:768].rearrange("p (b m) -> p b m", b=6)
        h32 = cst[:, 768:1536].rearrange("p (b m) -> p b m", b=6)
        ident = cst[:, 1536:1664]
        bias_rows = [sb(f"bias{n}", [128, 2, TW], F16) for n in (1, 2)]
        ones = sb("ones", [128, TT], F16)
        neg_half = sb("neg_half", [128, 4], F32)
        par = sb("par", [128, 12], F32)
        row1 = par[:, 11:12]
        ssq = [sb(f"ssq{n}", [TT, K, 2], F32) for n in (1, 2)]
        rs = [sb(f"rs{n}", [TT, K, 2], F32) for n in (1, 2)]
        bn = [sb(f"bn{n}", [128, 3, U, BND], F32) for n in (1, 2)]
        gst = [sb(f"gst{n}", [128, 2, 3], F32) for n in (1, 2)]
        gsq_ch = sb("gsq_ch", [128, 3], F32)
        gsq = sb("gsq", [128, 3], F32)
        gmu_b3 = sb("gmu_b3", [128, 3], F32)
        gmu = sb("gmu", [128, 3, 2], F32)
        gvar = sb("gvar", [128, 3], F32)
        gscale = [sb(f"gscale{n}", [128, 3], F32) for n in (1, 2)]
        gshift = [sb(f"gshift{n}", [128, 3, 2], F32) for n in (1, 2)]
        h_bias = sb("h_bias", [128, 3], F32)
        wsum = sb("wsum", [128, 8], F32)
        bsum = sb("bsum", [2, 2], F32)

        tm = [ctx.enter_context(nc.psum_tensor(f"tm{i}", [TT, 2, TW], F32)) for i in range(TM_BANKS)]
        tp = ctx.enter_context(nc.psum_tensor("tp", [128, 3, 512], F32))
        hp = ctx.enter_context(nc.psum_tensor("hp", [128, 512], F32))
        lp = ctx.enter_context(nc.psum_tensor("lp", [128, 512], F32))

        s_small = sem("biases_and_parameters_loaded")
        s_cload = sem("constants_loaded")
        s_wload = sem("weights_loaded")
        s_fill = sem("constant_fills_done")
        s_h16 = sem("hadamard_fp16_ready")
        s_wmean = sem("weight_means_ready")
        s_wcen = sem("weights_centred")
        s_whi = sem("weights_hi_ready")
        s_wlo = sem("weights_lo_ready")
        s_chain = sem("dve_chain")
        s_gn_chain = [sem("dve_chain_gn1"), sem("dve_chain_gn2")]
        s_load = [sem(f"x_unit{u}_loaded") for u in range(U)]
        s_xs32 = sem("pair0_xs32_ready")
        s_xs_hi, s_xs_lo = sem("xs_hi_ready"), sem("xs_lo_ready")
        s_h = sem("h_out_ready")
        s_res = sem("residual_done")
        s_bn = [sem("bn_stats_x"), sem("bn_stats_x1")]
        s_gst = sem("gn_stats_ready")
        s_gred = sem("gn_reduced")
        s_gread = sem("gn_psum_read")
        s_gvar = sem("gn_var_ready")
        s_grs = sem("gn_rstd_ready")
        s_gn = [sem("gn1_ready"), sem("gn2_ready")]
        s_hbias, s_bias = sem("h_bias_ready"), sem("layer1_bias_ready")
        s_x1_hi, s_x1_lo = sem("x1_hi_ready"), sem("x1_lo_ready")
        s_mm = [sem(f"mm{n}_done") for n in (1, 2)]
        s_ssq = [sem(f"ssq{n}_ready") for n in (1, 2)]
        s_rs = [sem(f"rstd{n}_ready") for n in (1, 2)]
        s_z = [sem(f"z{n}_ready") for n in (1, 2)]
        s_tp = [sem(f"transposed{n}") for n in (1, 2)]
        s_ge = [sem(f"gelu{n}_done") for n in (1, 2)]
        s_ge_hi = [sem(f"gelu_hi{n}_ready") for n in (1, 2)]
        s_ge_lo = [sem(f"gelu_lo{n}_ready") for n in (1, 2)]
        s_l3 = sem("l3_out_ready")
        s_fin = sem("out_ready")
        s_store = sem("stored")

        s_passed = {e.engine: sem(f"waits_passed_{n}")
                    for n, e in enumerate((nc.scalar, nc.vector, nc.gpsimd))}

        def later(value):
            return not isinstance(value, int) or value > 0

        def passed(eng, value):
            if not isinstance(value, int):
                eng.sem_inc(s_passed[eng.engine], 1)

        def xcols(p, b, u):
            return X[:, bass.ds((p % NX) * SLOT + b * BLK + u * UT, UT)]

        def freed(g, u):
            return g + 1 - {0: 1, 1: 3}.get(u, 2)

        def ge_buf(u, n):
            return 2 if n == 0 and u == U - 1 else u % 2

        def ge_freed(g, u, n):
            if n == 1:
                return freed(g, u)
            return g + 1 - {0: 3, 1: 3, U - 1: U}.get(u, 2)

        def prev(p, u, d):
            return U * p + u - d, (u - d) % U

        def exists(p, u, layer):
            if not isinstance(p, int):
                return True
            return 0 <= U * p + u + 1 - layer < U * PAIRS

        sums = {}

        def plus(p, d):
            if isinstance(p, int) or d == 0:
                return p + d
            if (id(p), d) not in sums:
                sums[id(p), d] = p, p + d
            return sums[id(p), d][1]

        def job(p, u, kind):
            at = (PLAN0 if isinstance(p, int) and p == 0 else PLAN)[u].get(kind)
            if at is None or isinstance(p, int) and p + at[0] >= PAIRS:
                return None
            return plus(p, at[0]), at[1]

        def step_before(p, u):
            return (p, u - 1) if u > 0 else (plus(p, -1), U - 1)

        def step_after(p, u):
            return (p, u + 1) if u < U - 1 else (plus(p, 1), 0)

        def split_next(p, u):
            if u < U - 1:
                return (p, u + 1) if exists(p, u + 1, 1) else None
            return (plus(p, 1), 0) if exists(p, u + 1, 1) else None

        def h_bank(q, c, b):
            if isinstance(q, int) and q == 0:
                return (hp, lp)[(3 * c + b) % 2], 1
            return hp, 0

        def tm_before(p, u, n, k):
            at = 8 * u + 4 * n + k
            while True:
                at -= TM_GAP[at % len(TM_GAP)]
                off = at % 8
                g = U * p + at // 8
                n0, k0 = off // 4, off % 4
                if isinstance(g, int):
                    if g < 0:
                        return None
                    if not 0 <= g - n0 < U * PAIRS:
                        continue
                return s_z[n0], K * (g - n0) + k0 + 1

        stage = X[:, 2 * SLOT:3 * SLOT]
        wst = [stage[:, n * 768:(n + 1) * 768].rearrange("p (b o) -> p b o", b=4) for n in (0, 1)]
        w12st = stage[:, 0:1536].rearrange("p (b o) -> p b o", b=8)
        w3st = stage[:, 1536:2304].rearrange("p (b o) -> p b o", b=6)
        bst = stage[:, 2304:2304 + 4 * C].rearrange("p (n i o) -> p n i o", n=2, i=2)
        bscr = stage[:, 2304 + 4 * C:2304 + 8 * C].rearrange("p (n i o) -> p n i o", n=2, i=2)
        xs32 = stage[:, 4096:4096 + 6 * UT].rearrange("p (a b t) -> p a b t", a=2, b=3)
        escr = stage[0:2, 2304 + 8 * C:2308 + 8 * C].rearrange("p (n i) -> p n i", n=2)

        block = ctx.enter_context(nc.Block())

        @block.sync
        def _(sp):
            def load(p, u):
                t0 = u * UT
                sp.dma_start(X[:, bass.ds((p % NX) * SLOT, 2 * BLK)].rearrange("c (i t) -> c i t", i=2)[:, :, t0:t0 + UT],
                             x[bass.ds(2 * p, 2), 0:CA, t0:t0 + UT].rearrange("i c t -> c i t")).then_inc(s_load[u], 16)
                for i in range(2):
                    sp.dma_start(X[i * CC:(i + 1) * CC, bass.ds((p % NX) * SLOT + 2 * BLK + t0, UT)],
                                 x[bass.ds(2 * p + i, 1), CA:C, t0:t0 + UT].rearrange("i c t -> c (i t)")
                                 ).then_inc(s_load[u], 16)

            def store(p, u):
                sp.wait_ge(s_fin, 3 * (U * p + u + 1))
                t0 = u * UT
                sp.dma_start(out[bass.ds(2 * p, 2), 0:CA, t0:t0 + UT].rearrange("i c t -> c i t"),
                             X[:, bass.ds((p % NX) * SLOT, 2 * BLK)].rearrange("c (i t) -> c i t", i=2)[:, :, t0:t0 + UT]
                             ).then_inc(s_store, 16)
                for i in range(2):
                    sp.dma_start(out[bass.ds(2 * p + i, 1), CA:C, t0:t0 + UT].rearrange("i c t -> c (i t)"),
                                 X[i * CC:(i + 1) * CC, bass.ds((p % NX) * SLOT + 2 * BLK + t0, UT)]
                                 ).then_inc(s_store, 16)

            sp.dma_start(par[:, :], params).then_inc(s_small, 16)
            sp.dma_start(bst[0:2].rearrange("p n i o -> p (n i o)"), biases).then_inc(s_small, 16)
            for u in range(U):
                load(0, u)
            sp.dma_start(cst[:, :], consts).then_inc(s_cload, 16)
            sp.dma_start(stage[:, 0:2304], weights).then_inc(s_wload, 16)
            for u in range(U):
                sp.wait_ge(s_load[u], 48)
                load(1, u)
            sp.wait_ge(s_wlo, 3)
            for u in range(U):
                sp.wait_ge(s_load[u], 96)
                load(2, u)

            with sp.Fori(0, PAIRS - NX) as p:
                for u in range(U):
                    store(p, u)
                    sp.wait_ge(s_store, 48 * (U * p + u + 1))
                    sp.wait_ge(s_load[u], 48 * (p + NX))
                    load(p + NX, u)
            with sp.Fori(PAIRS - NX, PAIRS) as p:
                for u in range(U):
                    store(p, u)
            sp.wait_ge(s_store, 48 * U * PAIRS)

        @block.tensor
        def _(pe):
            def gn_reduce(j):
                pe.wait_ge(s_gst, j + 1)
                for b, terms in enumerate((((AA, 0), (CIA, 2)), ((AA, 1), (CJA, 2)), ((AIC, 0), (AJC, 1), (CCB, 2)))):
                    for i, (m, src) in enumerate(terms):
                        last = nc.tensor.matmul(hp[:, 2 * b:2 * b + 2], group_mean[:, m, :], gst[j % 2][:, :, src],
                                                start=(i == 0), stop=(i == len(terms) - 1))
                last.then_inc(s_gred, 1)

            def gn1(q):
                if later(GREADS * q):
                    pe.wait_ge(s_gread, GREADS * q)
                gn_reduce(2 * q)

            def h_shift(q):
                pe.wait_ge(s_gread, GREADS * q + 1)
                pe.wait_ge(s_gn[0], q + 1)
                for b, terms in enumerate((((AA, 0), (CIA, 2)), ((AA, 1), (CJA, 2)), ((AIC, 0), (AJC, 1), (CCB, 2)))):
                    for i, (m, src) in enumerate(terms):
                        last = nc.tensor.matmul(hp[:, b:b + 1], h32[:, m, :], gshift[0][:, src, 0:1],
                                                start=(i == 0), stop=(i == len(terms) - 1))
                last.then_inc(s_gred, 1)

            def gn2(q):
                pe.wait_ge(s_res, 21 * (q + 1))
                gn_reduce(2 * q + 1)

            def w1_shift(q):
                pe.wait_ge(s_gread, GREADS * q + 3)
                pe.wait_ge(s_gn[1], q + 1)
                for i, terms in enumerate((((0, 0), (1, 2)), ((3, 1), (2, 2)))):
                    for r, (rows, src) in enumerate(terms):
                        last = nc.tensor.matmul(hp[0:2, i * C:(i + 1) * C], gshift[1][:, src, :], w32[:, rows, :],
                                                start=(r == 0), stop=(r == 1))
                last.then_inc(s_gred, 1)

            def groupnorm_means(q, n):
                (gn1, gn2)[n](q)

            def groupnorm_shift(q, n):
                (h_shift, w1_shift)[n](q)

            def h_out(q, c, b):
                a = U * q + c
                bank, ahead = h_bank(q, c, b)
                if b == 0:
                    pe.wait_ge(s_xs_lo, a + 1)
                if c == 0 and b == 0:
                    pe.wait_ge(s_gread, GREADS * q + 2)
                else:
                    if later(3 * a + b - ahead):
                        pe.wait_ge(s_res, 3 * a + b - ahead)
                hi, lo = xs_hi[:, c % 2], xs_lo[:, c % 2]
                if b < 2:
                    terms = [(AA, b, 0, 128), ((CIA, CJA)[b], 2, 0, 128)]
                else:
                    terms = [(CCB, 2, 0, 128), (AIC, 0, 0, 64), (AJC, 1, 64, 128)]
                n = 0
                for m, src, lo_p, hi_p in terms:
                    for part in (hi, lo):
                        last = nc.tensor.matmul(bank[lo_p:hi_p, 0:UT], h16[:, m, lo_p:hi_p], part[:, src, :],
                                                start=(n == 0), stop=(m in ((CIA, CJA) if b < 2 else (AIC, AJC)) and part is lo),
                                                skip_group_check=True)
                        n += 1
                last.then_inc(s_h, 1)

            def group(p, u, n, k):
                if not exists(p, u, n + 1):
                    return
                g, un = prev(p, u, n)
                if k == 0:
                    pe.wait_ge((s_x1_lo, s_ge_lo[0])[n], g + 1)
                    if n == 0 and u == 0:
                        pe.wait_ge(s_bias, p + 1)
                before = tm_before(p, u, n, k)
                if before:
                    pe.wait_ge(*before)
                dst = tm[TM_BANK[8 * u + 4 * n + k]]
                hi, lo = ((x1_hi, x1_lo), (ge_hi[0], ge_lo[0]))[n]
                buf = (un % 2, ge_buf(un, 0))[n]
                cols = slice(k * TT, (k + 1) * TT)
                nc.tensor.matmul(dst[:, :, :], ones[:, :], bias_rows[n][:, :, :], start=True, stop=False,
                                 skip_group_check=True)
                for act, w in ((hi, w_hi[n]), (hi, w_lo[n]), (lo, w_hi[n])):
                    nc.tensor.matmul(dst[:, :, 0:C], act[:, buf, 2, cols], w[:, 1:3, :], start=False, stop=False,
                                     skip_group_check=True)
                for i in range(2):
                    for r, (act, w) in enumerate(((hi, w_hi[n]), (hi, w_lo[n]), (lo, w_hi[n]))):
                        last = nc.tensor.matmul(dst[:, i, 0:C], act[:, buf, i, cols], w[:, 3 * i, :], start=False,
                                                stop=(r == 2), skip_group_check=True)
                last.then_inc(s_mm[n], 1)

            def transposes(p, u, n, k):
                if not exists(p, u, n + 1):
                    return
                g, _ = prev(p, u, n)
                if k == 0:
                    if n == 0:
                        if later(2 * (g - 1)):
                            pe.wait_ge(s_ge[1], 2 * (g - 1))
                    else:
                        pe.wait_ge(s_ge[0], 2 * min(g + 2, U * PAIRS) if isinstance(g, int) else 2 * (g + 2))
                pe.wait_ge(s_z[n], K * g + k + 1)
                cols = slice(k * TT, (k + 1) * TT)
                for blk, at in ((0, 0), (1, C + CC), (2, CA)):
                    last = nc.tensor.transpose(tp[:, blk, cols], z[n][:, k, at:at + 128], ident[0:TT, 0:TT])
                if k == K - 1:
                    last.then_inc(s_tp[n], 1)

            def l3_out(p, u, b):
                if not exists(p, u, 3):
                    return
                g, u3 = prev(p, u, 2)
                if b == 0:
                    pe.wait_ge(s_ge_lo[1], g + 1)
                if later(3 * g + b):
                    pe.wait_ge(s_fin, 3 * g + b)
                hi, lo = ge_hi[1][:, ge_buf(u3, 1)], ge_lo[1][:, ge_buf(u3, 1)]
                if b < 2:
                    terms = [(AA, b, 0, 128), ((CIA, CJA)[b], 2, 0, 128)]
                else:
                    terms = [(CCB, 2, 0, 128), (AIC, 0, 0, 64), (AJC, 1, 64, 128)]
                ends = (CIA, CJA) if b < 2 else (AIC, AJC)
                n = 0
                for m, src, lo_p, hi_p in terms:
                    for r, (w, act) in enumerate(((w3_hi, hi), (w3_hi, lo), (w3_lo, hi))):
                        last = nc.tensor.matmul(lp[lo_p:hi_p, 0:UT], w[:, m, lo_p:hi_p], act[:, src, :],
                                                start=(n == 0), stop=(m in ends and r == 2), skip_group_check=True)
                        n += 1
                last.then_inc(s_l3, 1)

            def step(p, u):
                last = step_before(p, u)
                h, h_2nd, gn, gn_2nd = (
                    job(p, u, kind) for kind in (
                        "h", "h_2nd", "gn", "gn_2nd"))
                group(p, u, 0, 0)
                group(p, u, 0, 1)
                transposes(*last, 1, 2)
                transposes(*last, 1, 3)
                if gn:
                    groupnorm_means(*gn)
                group(p, u, 0, 2)
                group(p, u, 0, 3)
                if h:
                    h_out(*h, 0)
                transposes(p, u, 0, 0)
                if gn:
                    groupnorm_shift(*gn)
                group(p, u, 1, 0)
                group(p, u, 1, 1)
                if gn_2nd:
                    groupnorm_means(*gn_2nd)
                transposes(p, u, 0, 1)
                transposes(p, u, 0, 2)
                transposes(p, u, 0, 3)
                group(p, u, 1, 2)
                if h:
                    h_out(*h, 1)
                l3_out(p, u, 0)
                if gn_2nd:
                    groupnorm_shift(*gn_2nd)
                if h:
                    h_out(*h, 2)
                transposes(p, u, 1, 0)
                l3_out(p, u, 1)
                if h_2nd:
                    h_out(*h_2nd, 0)
                group(p, u, 1, 3)
                if h_2nd:
                    h_out(*h_2nd, 1)
                transposes(p, u, 1, 1)
                if h_2nd:
                    h_out(*h_2nd, 2)
                l3_out(p, u, 2)

            pe.wait_ge(s_cload, 16)
            gn1(0)
            h_shift(0)
            pe.wait_ge(s_h16, 1)
            for c in range(U):
                for b in range(3):
                    h_out(0, c, b)
            gn2(0)
            pe.wait_ge(s_wcen, 1)
            w1_shift(0)
            pe.wait_ge(s_fill, 1)
            pe.wait_ge(s_wlo, 3)
            run(pe, step)

        @block.scalar
        def _(act):
            def scaled_hi(q, c, b):
                a = U * q + c
                if c == 0 and b == 0:
                    act.wait_ge(s_gn[0], q + 1)
                if b == 0 and later(3 * freed(a, c)):
                    act.wait_ge(s_h, 3 * freed(a, c))
                    passed(act, 3 * freed(a, c))
                ins = nc.scalar.activation(xs_hi[:, c % 2, b, :], xcols(q, b, c), ACT.Copy,
                                           scale=gscale[0][:, b:b + 1])
                if b == 2:
                    ins.then_inc(s_xs_hi, 1)

            def split_x1(p, u, b):
                g = U * p + u
                if u == 0 and b == 0:
                    act.wait_ge(s_gn[1], p + 1)
                if b == 0 and later(K * freed(g, u)):
                    act.wait_ge(s_mm[0], K * freed(g, u))
                    passed(act, K * freed(g, u))
                ins = nc.scalar.activation(x1_hi[:, u % 2, b, :], xcols(p, b, u), ACT.Copy,
                                           scale=gscale[1][:, b:b + 1])
                if b == 2:
                    ins.then_inc(s_x1_hi, 1)

            def squares(p, u, n, k):
                if not exists(p, u, n + 1):
                    return
                g, _ = prev(p, u, n)
                act.wait_ge(s_mm[n], K * g + k + 1)
                for i in range(2):
                    last = nc.scalar.activation(z[n][:, k, i * TW:(i + 1) * TW], tm[TM_BANK[8 * u + 4 * n + k]][:, i, :], ACT.Square,
                                                scale=float(C) ** -0.5,
                                                accum_out=ssq[n][:, k, i:i + 1])
                last.then_inc(s_ssq[n], 1)

            def gelu(p, u, n):
                if not exists(p, u, n + 1):
                    return
                g, _ = prev(p, u, n)
                act.wait_ge(s_tp[n], g + 1)
                if later(g):
                    act.wait_ge(s_ge_lo[n], g)
                for blocks, c in ((slice(0, 2), 0), (slice(2, 3), 1)):
                    nc.scalar.activation(ge[n][:, blocks, :], tp[:, blocks, 0:UT], ACT.Gelu,
                                         bias=par[:, 4 * n + 2 + c:4 * n + 3 + c],
                                         scale=par[:, 4 * n + c:4 * n + c + 1]).then_inc(s_ge[n], 1)

            def gelu_hi(p, u, n):
                if not exists(p, u, n + 1):
                    return
                g, un = prev(p, u, n)
                act.wait_ge(s_ge[n], 2 * (g + 1))
                if later((K, 3)[n] * ge_freed(g, un, n)):
                    act.wait_ge((s_mm[1], s_l3)[n], (K, 3)[n] * ge_freed(g, un, n))
                nc.scalar.activation(ge_hi[n][:, ge_buf(un, n)], ge[n][:, :, :], ACT.Copy).then_inc(s_ge_hi[n], 1)

            def step(p, u):
                last = step_before(p, u)
                split = split_next(p, u)
                hi, hi_end = (
                    job(p, u, kind) for kind in (
                        "hi", "hi_end"))
                gelu_hi(*last, 0)
                if split and u < U - 1:
                    split_x1(*split, 0)
                squares(*last, 1, 2)
                if split and u < U - 1:
                    split_x1(*split, 1)
                squares(*last, 1, 3)
                if hi:
                    scaled_hi(*hi, 0)
                    scaled_hi(*hi, 1)
                if split and u < U - 1:
                    split_x1(*split, 2)
                squares(p, u, 0, 0)
                if hi:
                    scaled_hi(*hi, 2)
                squares(p, u, 0, 1)
                gelu(*last, 1)
                squares(p, u, 0, 2)
                squares(p, u, 0, 3)
                gelu_hi(*last, 1)
                if split and u == U - 1:
                    for b in range(3):
                        split_x1(*split, b)
                squares(p, u, 1, 0)
                squares(p, u, 1, 1)
                gelu(p, u, 0)
                if hi_end:
                    for b in range(3):
                        scaled_hi(*hi_end, b)

            def centre(n):
                act.wait_ge(s_wmean, 2)
                for b in range(4):
                    last = nc.scalar.activation((w32, wst[1])[n][:, b, :], wst[n][:, b, :], ACT.Identity,
                                                bias=wsum[:, 4 * n + b:4 * n + b + 1], scale=W_SCALE)
                last.then_inc(s_wcen, 1)

            def weights_hi(n):
                act.wait_ge(s_wcen, n + 1)
                nc.scalar.activation((w_hi[0], w_hi[1], w3_hi)[n][:, :, :], (w32[:, :, :], wst[1], w3st)[n],
                                     ACT.Copy).then_inc(s_whi, 1)

            def first_hi(c):
                if c == 0:
                    act.wait_ge(s_gn[0], 1)
                if c >= 2:
                    act.wait_ge(s_xs_lo, c - 1)
                for b in range(3):
                    last = nc.scalar.activation(xs32[:, c % 2, b, :], xcols(0, b, c), ACT.Copy,
                                                scale=gscale[0][:, b:b + 1])
                last.then_inc(s_xs32, 1)
                if c >= 2:
                    act.wait_ge(s_h, 3 * (c - 1))
                act.wait_ge(s_xs32, c + 1)
                nc.scalar.activation(xs_hi[:, c % 2], xs32[:, c % 2], ACT.Copy).then_inc(s_xs_hi, 1)

            act.wait_ge(s_small, 32)
            act.wait_ge(s_cload, 16)
            nc.scalar.activation(h16[:, :, :], h32, ACT.Copy).then_inc(s_h16, 1)
            for c in range(U):
                first_hi(c)
            for n in range(2):
                centre(n)
                weights_hi(n)
            nc.scalar.activation(w3st, w3st, ACT.Copy, scale=W_SCALE).then_inc(s_wcen, 1)
            weights_hi(2)
            for b in range(3):
                split_x1(0, 0, b)
            run(act, step)

        @block.gpsimd
        def _(pool):
            def groupnorm_rstd(q, n):
                pool.wait_ge(s_gvar, 2 * q + n + 1)
                nc.gpsimd.tensor_tensor(gscale[n][:, :], gvar[:, :], neg_half[:, 0:3], ALU.pow).then_inc(s_grs, 1)

            def rstd(p, u, n, k):
                if not exists(p, u, n + 1):
                    return
                g, _ = prev(p, u, n)
                pool.wait_ge(s_ssq[n], K * g + k + 1)
                nc.gpsimd.tensor_tensor(rs[n][:, k, :], ssq[n][:, k, :], neg_half[0:TT, 0:2],
                                        ALU.pow).then_inc(s_rs[n], 1)

            def gelu_lo(p, u, n, b):
                if not exists(p, u, n + 1):
                    return
                g, un = prev(p, u, n)
                if b == 0:
                    pool.wait_ge(s_ge_hi[n], g + 1)
                ins = nc.gpsimd.tensor_tensor(ge_lo[n][:, ge_buf(un, n), b, :], ge[n][:, b, :],
                                              ge_hi[n][:, ge_buf(un, n), b, :], ALU.subtract)
                if b == 2:
                    ins.then_inc(s_ge_lo[n], 1)

            def step(p, u):
                last = step_before(p, u)
                gn, gn_2nd = (
                    job(p, u, kind) for kind in (
                        "gn", "gn_2nd"))
                rstd(*last, 1, 3)
                gelu_lo(*last, 0, 1)
                rstd(p, u, 0, 0)
                rstd(p, u, 0, 1)
                if gn:
                    groupnorm_rstd(*gn)
                gelu_lo(*last, 0, 2)
                rstd(p, u, 0, 2)
                rstd(p, u, 0, 3)
                gelu_lo(*last, 1, 0)
                gelu_lo(*last, 1, 1)
                gelu_lo(*last, 1, 2)
                if gn_2nd:
                    groupnorm_rstd(*gn_2nd)
                rstd(p, u, 1, 0)
                rstd(p, u, 1, 1)
                gelu_lo(p, u, 0, 0)
                rstd(p, u, 1, 2)

            def first_lo(c):
                pool.wait_ge(s_xs_hi, c + 1)
                for b in range(3):
                    last = nc.gpsimd.tensor_tensor(xs_lo[:, c % 2, b, :], xs32[:, c % 2, b, :],
                                                   xs_hi[:, c % 2, b, :], ALU.subtract)
                last.then_inc(s_xs_lo, 1)

            pool.wait_ge(s_fill, 1)
            groupnorm_rstd(0, 0)
            for c in range(U):
                first_lo(c)
            for n in range(2):
                pool.wait_ge(s_whi, n + 1)
                nc.gpsimd.tensor_tensor(w_lo[n][:, :, :], (w32[:, :, :], wst[1])[n], w_hi[n][:, :, :],
                                        ALU.subtract).then_inc(s_wlo, 1)
            groupnorm_rstd(0, 1)
            pool.wait_ge(s_whi, 3)
            nc.gpsimd.tensor_tensor(w3_lo[:, :, :], w3st, w3_hi[:, :, :], ALU.subtract).then_inc(s_wlo, 1)
            run(pool, step)

        @block.vector
        def _(dve):
            links = {"at": 0}

            def link(ins):
                links["at"] += 1
                ins.then_inc(s_chain, 1)
                dve.wait_ge(s_chain, links["at"])

            def fills():
                for n in range(2):
                    nc.vector.memset(bias_rows[n][:, :, :], 0.0)
                nc.vector.memset(ones[:, :], 1.0)
                nc.vector.memset(neg_half[:, :], -0.5).then_inc(s_fill, 1)
                dve.wait_ge(s_fill, 1)

            def split_bias(n, value, scratch):
                dst = bias_rows[n][0:2, :, 0:C]
                link(nc.vector.tensor_copy(dst, value))
                link(nc.vector.scalar_tensor_tensor(out=scratch, in0=dst, scalar=row1[0:2, :], in1=value,
                                                    op0=ALU.mult, op1=ALU.subtract))
                link(nc.vector.tensor_scalar(dst, scratch, -1.0, None, ALU.mult))

            def layer_biases():
                dve.wait_ge(s_small, 32)
                link(nc.vector.reduce_sum(bsum[:, :], bst[0:2, :, 0, :], axis=AX.X))
                link(nc.vector.tensor_scalar(bsum[:, :], bsum[:, :], -1.0 / C, None, ALU.mult))
                nc.vector.tensor_scalar(b32[:, :, :], bst[0:2, 0], bsum[:, 0:1], W_SCALE, ALU.add, ALU.mult)
                link(nc.vector.tensor_scalar(bscr[0:2, 0], bst[0:2, 1], bsum[:, 1:2], W_SCALE, ALU.add, ALU.mult))
                split_bias(1, bscr[0:2, 0], bscr[0:2, 1])
                link(nc.vector.memset(escr[:, 0], (C * LN_EPS) ** 0.5 * W_SCALE))
                link(nc.vector.tensor_copy(bias_rows[0][0:2, :, C], escr[:, 0]))
                link(nc.vector.scalar_tensor_tensor(out=escr[:, 1], in0=bias_rows[0][0:2, :, C], scalar=row1[0:2, :],
                                                    in1=escr[:, 0], op0=ALU.mult, op1=ALU.subtract))
                for n in range(2):
                    last = nc.vector.tensor_scalar(bias_rows[n][0:2, :, C], escr[:, 1], -1.0, None, ALU.mult)
                link(last)

            def weight_means():
                dve.wait_ge(s_wload, 16)
                nc.vector.reduce_sum(wsum[:, :], w12st, axis=AX.X).then_inc(s_wmean, 1)
                dve.wait_ge(s_wmean, 1)
                nc.vector.tensor_scalar(wsum[:, :], wsum[:, :], -W_SCALE / C, None, ALU.mult).then_inc(s_wmean, 1)

            def first_stats():
                for c in range(U):
                    dve.wait_ge(s_load[c], 48)
                    for b in range(3):
                        last = nc.vector.bn_stats(bn[0][:, b, c, :], xcols(0, b, c))
                    last.then_inc(s_bn[0], 1)

            def stats_x(q, first, last):
                for at in range(first, last):
                    if at % 3 == 0:
                        dve.wait_ge(s_load[at // 3], 48 * (q + 1))
                        passed(dve, 48 * (q + 1))
                    ins = nc.vector.bn_stats(bn[0][:, at % 3, at // 3, :], xcols(q, at % 3, at // 3))
                    if at % 3 == 2:
                        ins.then_inc(s_bn[0], 1)

            def scaled_lo(q, c, b):
                if b == 0:
                    dve.wait_ge(s_xs_hi, U * q + c + 1)
                ins = nc.vector.scalar_tensor_tensor(out=xs_lo[:, c % 2, b, :], in0=xcols(q, b, c),
                                                     scalar=gscale[0][:, b:b + 1], in1=xs_hi[:, c % 2, b, :],
                                                     op0=ALU.mult, op1=ALU.subtract)
                if b == 2:
                    ins.then_inc(s_xs_lo, 1)

            def residual(q, c, b):
                r = 3 * (U * q + c) + b + 1
                dve.wait_ge(s_h, r)
                nc.vector.scalar_tensor_tensor(out=xcols(q, b, c), in0=h_bank(q, c, b)[0][:, 0:UT], scalar=h_bias[:, b:b + 1],
                                               in1=xcols(q, b, c), op0=ALU.add, op1=ALU.add).then_inc(s_res, 1)

            def stats_x1(q, c, b):
                r = 3 * (U * q + c) + b + 1
                dve.wait_ge(s_res, r)
                passed(dve, r)
                ins = nc.vector.bn_stats(bn[1][:, b, c, :], xcols(q, b, c))
                if b == 2:
                    ins.then_inc(s_bn[1], 1)

            LINKS = ((2, 2, 0, 0), (3, 2, 1, 2))

            def chain(q, n, stage):
                first = sum(LINKS[n]) * q + sum(LINKS[n][:stage])
                at = [0]

                def do(ins):
                    at[0] += 1
                    ins.then_inc(s_gn_chain[n], 1)
                    dve.wait_ge(s_gn_chain[n], first + at[0])

                return do

            def gn_stats(q, n):
                do = chain(q, n, 0)
                dve.wait_ge(s_bn[n], U * (q + 1))
                passed(dve, U * (q + 1))
                for b in range(3):
                    last = nc.vector.bn_aggr(gst[n][:, :, b], bn[n][:, b, :, :].rearrange("p u s -> p (u s)"))
                do(last)
                if n == 1:
                    do(nc.vector.tensor_tensor(gst[n][:, 0, :], gst[n][:, 0, :], par[:, 8:11], ALU.subtract))
                do(nc.vector.tensor_tensor(gsq_ch[:, :], gst[n][:, 0, :], gst[n][:, 0, :], ALU.mult))
                nc.vector.tensor_tensor(gst[n][:, 1, :], gst[n][:, 1, :], gsq_ch[:, :], ALU.add).then_inc(s_gst, 1)

            def gn_var(q, n):
                do = chain(q, n, 1)
                reads = GREADS * q + 2 * n + 1
                dve.wait_ge(s_gred, reads)
                nc.vector.tensor_copy(gmu[:, :, :], hp[:, 0:6].rearrange("p (b s) -> p b s", b=3)).then_inc(s_gread, 1)
                dve.wait_ge(s_gread, reads)
                do(nc.vector.tensor_tensor(gsq[:, :], gmu[:, :, 0], gmu[:, :, 0], ALU.mult))
                do(nc.vector.tensor_tensor(gvar[:, :], gmu[:, :, 1], gsq[:, :], ALU.subtract))
                nc.vector.tensor_scalar(gvar[:, :], gvar[:, :], 0.0, GN_EPS, ALU.max, ALU.add).then_inc(s_gvar, 1)

            def gn_shift(q, n):
                do = chain(q, n, 2)
                dve.wait_ge(s_grs, 2 * q + n + 1)
                mu = gmu[:, :, 0]
                if n == 1:
                    do(nc.vector.tensor_tensor(gmu_b3[:, :], mu, par[:, 8:11], ALU.add))
                    mu = gmu_b3[:, :]
                for i in range(2):
                    last = nc.vector.scalar_tensor_tensor(out=gshift[n][:, :, i], in0=mu, scalar=-1.0,
                                                          in1=gscale[n][:, :], op0=ALU.mult, op1=ALU.mult)
                last.then_inc(s_gn[n], 1)

            def gn_bias(q, n):
                reads = GREADS * q + 2 * n + 2
                dve.wait_ge(s_gred, reads)
                if n == 0:
                    nc.vector.tensor_tensor(h_bias[:, :], hp[:, 0:3], par[:, 8:11], ALU.add).then_inc(s_gread, 1)
                    dve.wait_ge(s_gread, reads)
                    return
                do = chain(q, n, 3)
                nc.vector.tensor_tensor(b_row[:, :, :], hp[0:2, 0:2 * C].rearrange("p (i o) -> p i o", i=2),
                                        b32[:, :, :], ALU.add).then_inc(s_gread, 1)
                dve.wait_ge(s_gread, reads)
                dst = bias_rows[0][0:2, :, 0:C]
                do(nc.vector.tensor_copy(dst, b_row[:, :, :]))
                do(nc.vector.scalar_tensor_tensor(out=b_row[:, :, :], in0=dst, scalar=row1[0:2, :], in1=b_row[:, :, :],
                                                  op0=ALU.mult, op1=ALU.subtract))
                nc.vector.tensor_scalar(dst, b_row[:, :, :], -1.0, None, ALU.mult).then_inc(s_bias, 1)

            def x1_split_lo(p, u, b):
                if b == 0:
                    dve.wait_ge(s_x1_hi, U * p + u + 1)
                ins = nc.vector.scalar_tensor_tensor(out=x1_lo[:, u % 2, b, :], in0=xcols(p, b, u),
                                                     scalar=gscale[1][:, b:b + 1], in1=x1_hi[:, u % 2, b, :],
                                                     op0=ALU.mult, op1=ALU.subtract)
                if b == 2:
                    ins.then_inc(s_x1_lo, 1)

            def normalise(p, u, n, k):
                if not exists(p, u, n + 1):
                    return
                g, _ = prev(p, u, n)
                dve.wait_ge(s_rs[n], K * g + k + 1)
                nc.vector.tensor_tensor(z[n][:, k, 0:2 * C].rearrange("p (i o) -> p i o", i=2),
                                        tm[TM_BANK[8 * u + 4 * n + k]][:, :, 0:C],
                                        rs[n][:, k, :].unsqueeze(2).to_broadcast([TT, 2, C]),
                                        ALU.mult).then_inc(s_z[n], 1)

            def final(p, u, b):
                if not exists(p, u, 3):
                    return
                g, u3 = prev(p, u, 2)
                pp = p if u >= 2 else p - 1
                dve.wait_ge(s_l3, 3 * g + b + 1)
                nc.vector.scalar_tensor_tensor(out=xcols(pp, b, u3), in0=lp[:, 0:UT], scalar=1.0 / W_SCALE,
                                               in1=xcols(pp, b, u3), op0=ALU.mult, op1=ALU.add).then_inc(s_fin, 1)

            def step(p, u):
                last = step_before(p, u)
                split = split_next(p, u)
                h, h_2nd, hi, hi_end, gn, gn_2nd, gn_end, stats, stats_early = (
                    job(p, u, kind) for kind in (
                        "h", "h_2nd", "hi", "hi_end", "gn", "gn_2nd", "gn_end", "stats", "stats_early"))
                gn_next = job(*step_after(p, u), "gn")

                def stats_part(i):
                    if stats:
                        first, end = stats[1]
                        stats_x(stats[0], first + (end - first) * i // 3, first + (end - first) * (i + 1) // 3)

                if split and u < U - 1:
                    x1_split_lo(*split, 0)
                if stats_early:
                    stats_x(stats_early[0], *stats_early[1])
                if split and u < U - 1:
                    x1_split_lo(*split, 1)
                if gn_end:
                    gn_bias(*gn_end)
                normalise(p, u, 0, 0)
                if gn:
                    gn_var(*gn)
                if gn_2nd:
                    gn_stats(*gn_2nd)
                if split and u < U - 1:
                    x1_split_lo(*split, 2)
                if gn:
                    gn_shift(*gn)
                stats_part(0)
                normalise(p, u, 0, 1)
                if hi:
                    scaled_lo(*hi, 0)
                normalise(p, u, 0, 2)
                if h:
                    residual(*h, 0)
                if gn:
                    gn_bias(*gn)
                normalise(p, u, 0, 3)
                if hi:
                    scaled_lo(*hi, 1)
                if gn_2nd:
                    gn_var(*gn_2nd)
                if h:
                    stats_x1(*h, 0)
                if hi:
                    scaled_lo(*hi, 2)
                stats_part(1)
                stats_part(2)
                if h:
                    residual(*h, 1)
                if gn_2nd:
                    gn_shift(*gn_2nd)
                normalise(p, u, 1, 0)
                final(p, u, 0)
                if split and u == U - 1:
                    for b in range(3):
                        x1_split_lo(*split, b)
                normalise(p, u, 1, 1)
                if h:
                    residual(*h, 2)
                    stats_x1(*h, 1)
                final(p, u, 1)
                if hi_end:
                    for b in range(3):
                        scaled_lo(*hi_end, b)
                if h_2nd:
                    residual(*h_2nd, 0)
                    stats_x1(*h_2nd, 0)
                normalise(p, u, 1, 2)
                if h_2nd:
                    residual(*h_2nd, 1)
                if h:
                    stats_x1(*h, 2)
                if h_2nd:
                    stats_x1(*h_2nd, 1)
                    residual(*h_2nd, 2)
                normalise(p, u, 1, 3)
                if h_2nd:
                    stats_x1(*h_2nd, 2)
                final(p, u, 2)
                if gn_next:
                    gn_stats(*gn_next)

            fills()
            layer_biases()
            first_stats()
            for part in (gn_stats, gn_var, gn_shift, gn_bias):
                part(0, 0)
            for c in range(U):
                for b in range(3):
                    residual(0, c, b)
                    if 2 <= c <= 5:
                        stats_x(1, 3 * (c - 2) + b, 3 * (c - 2) + b + 1)
                    if c > 0:
                        stats_x1(0, c - 1, b)
                if c == 0:
                    weight_means()
            for b in range(3):
                stats_x1(0, U - 1, b)
            gn_stats(0, 1)
            stats_x(1, 12, 16)
            gn_var(0, 1)
            stats_x(1, 16, 17)
            gn_shift(0, 1)
            stats_x(1, 17, 21)
            for b in range(3):
                x1_split_lo(0, 0, b)
            gn_bias(0, 1)
            gn_stats(1, 0)
            run(dve, step)


def run(eng, step):
    for u in range(U):
        step(0, u)
    with eng.Fori(1, PAIRS - 2) as p:
        for u in range(U):
            step(p, u)
    for p in (PAIRS - 2, PAIRS - 1):
        for u in range(U):
            step(p, u)
    for u in range(2):
        step(PAIRS, u)


def blocks6(m):
    r = np.zeros((128, 6, 128), np.float32)
    r[:, AA] = m[:CA, :CA]
    r[:CC, CIA] = m[CA:, :CA]
    r[CC:, CJA] = m[CA:, :CA]
    r[:, AIC, :CC] = m[:CA, CA:]
    r[:, AJC, CC:] = m[:CA, CA:]
    r[:CC, CCB, :CC] = m[CA:, CA:]
    r[CC:, CCB, CC:] = m[CA:, CA:]
    return r.reshape(128, 768)


def blocks4(m):
    j = np.concatenate([m[:, CA:], m[:, :CA]], axis=1)
    r = np.zeros((128, 4, C), np.float32)
    r[:, 0] = m[:CA]
    r[:CC, 1] = m[CA:]
    r[CC:, 2] = j[CA:]
    r[:, 3] = j[:CA]
    return r.reshape(128, 4 * C)


def bias_layout(b1, b2):
    r = np.concatenate([p for b in (b1, b2) for p in (b, b[CA:], b[:CA])])
    return np.ascontiguousarray(np.broadcast_to(r, (2, 4 * C)))


def param_layout(g1, be1, g2, be2, b3):
    cols = [c for v in (g1, be1, g2, be2) for c in (v[:CA], np.tile(v[CA:], 2))]
    cols += [b3[:CA], b3[:CA], np.tile(b3[CA:], 2), (np.arange(128) == 1).astype(np.float32)]
    return np.ascontiguousarray(np.stack(cols, axis=1))


def constants():
    had = np.array([[1.0]], np.float32)
    while had.shape[0] < 256:
        had = np.block([[had, had], [had, -had]])
    had = (had / 16.0)[:C, :C].astype(np.float32)
    ch = np.arange(C)
    grp = (ch[:, None] // GROUP == ch[None, :] // GROUP).astype(np.float32) / np.float32(GROUP)
    return np.concatenate([blocks6(grp), blocks6(had), np.eye(128, dtype=np.float32)], axis=1)


def kernel(x, L1_conv_W1, L1_conv_b1, L1_conv_g1, L1_conv_beta1, L1_conv_W2, L1_conv_b2,
           L1_conv_g2, L1_conv_beta2, L1_conv_W3, L1_conv_b3):
    import concourse.bacc as bacc
    from concourse.bass_utils import run_bass_kernel_spmd

    x = np.asarray(x)
    w1t, w2t, w3t = (np.asarray(w).T for w in (L1_conv_W1, L1_conv_W2, L1_conv_W3))
    arrays = {
        "x": np.ascontiguousarray(x.reshape(B, C, HW)),
        "weights": np.concatenate([blocks4(w1t), blocks4(w2t), blocks6(w3t)], axis=1),
        "biases": bias_layout(np.asarray(L1_conv_b1), np.asarray(L1_conv_b2)),
        "params": param_layout(np.asarray(L1_conv_g1), np.asarray(L1_conv_beta1), np.asarray(L1_conv_g2),
                               np.asarray(L1_conv_beta2), np.asarray(L1_conv_b3)),
        "consts": constants(),
    }
    nc = bacc.Bacc("TRN2", target_bir_lowering=False, num_devices=1)
    args = [nc.dram_tensor(n, a.shape, mybir.dt.from_np(a.dtype), kind="ExternalInput").ap()
            for n, a in arrays.items()]
    out = nc.dram_tensor("out", (B, C, HW), F32, kind="ExternalOutput").ap()
    build(nc, *args, out)
    r = run_bass_kernel_spmd(nc, [arrays], core_ids=[0])
    return r.results[0]["out"].reshape(x.shape)
```
